# Optimizing a Trainium2 kernel written in Bass

```python
import numpy as np
import jax
import jax.numpy as jnp

def _softmax(x, axis=-1):
    return jax.nn.softmax(x, axis=axis)

def _gelu(x):
    return jax.nn.gelu(x, approximate=True)

def _silu(x):
    return jax.nn.silu(x)

def _sigmoid(x):
    return jax.nn.sigmoid(x)

def _layernorm(x, axis=-1, eps=1e-05):
    m = jnp.mean(x, axis=axis, keepdims=True)
    v = jnp.var(x, axis=axis, keepdims=True)
    return (x - m) / jnp.sqrt(v + eps)

def _scatter_add(tgt, idx, src, axis=0):
    return tgt.at[idx].add(src)

def _segment_sum(src, seg, n):
    return jax.ops.segment_sum(src, seg, n)
kernel_name = 'mk_xattn_seq_d4_seqx_r4_1c3ea0'

def setup_inputs(seed: int=0):
    np.random.seed(seed)
    _w = jnp.asarray

    def _rec_inputs():
        import jax
        import jax.numpy as jnp
        _rk = jax.random.key(seed)
        x = -0.0002928 + 1 * jax.random.normal(jax.random.fold_in(_rk, 1), (16, 256, 512), jnp.float32)
        _lenS = 256 - jax.random.randint(jax.random.fold_in(_rk, 7), (16,), 0, max(1, 256 // 4) + 1, jnp.int32)
        _lenS2 = 256 - jax.random.randint(jax.random.fold_in(_rk, 8), (16,), 0, max(1, 256 // 4) + 1, jnp.int32)
        _ctx_2048P = jax.random.normal(jax.random.fold_in(_rk, 12), (16, 16, 512), jnp.float32)
        _ctx_2048c = jax.random.dirichlet(jax.random.fold_in(_rk, 512), 0.3 * jnp.ones((16,), jnp.float32), (16, 256))
        _ctx_2048t = jnp.einsum('bsk,bkd->bsd', _ctx_2048c, _ctx_2048P)
        _ctx_2048t = _ctx_2048t * jax.lax.rsqrt(jnp.mean(jnp.square(_ctx_2048t)) + 1e-12) * 0.953939
        ctx_2048 = -1.39393e-06 + 0.999914 * (_ctx_2048t + 0.3 * jax.random.normal(jax.random.fold_in(_rk, 612), (16, 256, 512), jnp.float32))
        _validS = jnp.arange(256)[None, :] < _lenS[:, None]
        _validS2 = jnp.arange(256)[None, :] < _lenS2[:, None]
        _causal = jnp.tril(jnp.ones((256, 256), dtype=bool))
        mask_Bx1x2048_bf1 = jnp.ones((16, 1, 512), dtype=bool)
        mask_BxS2_bf1 = jnp.ones((16, 256), dtype=bool)
        mask_Bx1xSxS2_ff0 = jnp.where(jnp.ones((16, 1, 256, 256), dtype=bool), 0.0, -1000000000.0).astype(jnp.float32)
        return (x, ctx_2048, mask_Bx1x2048_bf1, mask_BxS2_bf1, mask_Bx1xSxS2_ff0)
    x, ctx_2048, mask_Bx1x2048_bf1, mask_BxS2_bf1, mask_Bx1xSxS2_ff0 = _rec_inputs()

    def _L0_xattn_setup():
        import jax, jax.numpy as jnp
        import numpy as np
        import math
        N_HEADS = 16
        EPS = 1e-05

        def _masked_instance_norm(x, mask):
            m = mask.astype(x.dtype)
            x = x * m
            n_valid = jnp.sum(m, axis=-1, keepdims=True)
            mean = jnp.sum(x, axis=-1, keepdims=True) / n_valid
            var = jnp.sum(x * x, axis=-1, keepdims=True) / n_valid - mean * mean
            x = (x - mean) / jnp.sqrt(jax.nn.relu(var) + EPS)
            return x * m
        key = jax.random.key(seed)
        ks = jax.random.split(key, 8)
        bs, c, t1, t2 = (2, 256, 512, 512)
        s = 1.0 / math.sqrt(c)
        return {'x': jax.random.normal(ks[0], (bs, c, t1), jnp.float32), 'mask': jnp.ones((bs, 1, t1), jnp.bool_), 'kv': jax.random.normal(ks[1], (bs, c, t2), jnp.float32), 'kv_mask': jnp.ones((bs, 1, t2), jnp.bool_), 'Wq': jax.random.normal(ks[2], (c, c), jnp.float32) * s, 'bq': jnp.zeros((c,), jnp.float32), 'Wk': jax.random.normal(ks[3], (c, c), jnp.float32) * s, 'bk': jnp.zeros((c,), jnp.float32), 'Wv': jax.random.normal(ks[4], (c, c), jnp.float32) * s, 'bv': jnp.zeros((c,), jnp.float32)}
    _L0_xattn_all = _L0_xattn_setup()
    _L0_xattn_in = {k: v for k, v in _L0_xattn_all.items() if k in ('Wq', 'bq', 'Wk', 'bk', 'Wv', 'bv')}
    del _L0_xattn_all

    def _L1_xattn_setup():
        import jax, jax.numpy as jnp
        import numpy as np
        HIDDEN = 512
        HEADS = 16
        HEAD_DIM = HIDDEN // HEADS
        LN_EPS = 1e-05
        GATE_INIT = 0.5

        def _layer_norm(x, gamma, beta):
            mu = jnp.mean(x, axis=-1, keepdims=True)
            var = jnp.mean(jnp.square(x - mu), axis=-1, keepdims=True)
            return (x - mu) * jax.lax.rsqrt(var + LN_EPS) * gamma + beta
        key = jax.random.key(seed)
        ks = jax.random.split(key, 8)
        B, T_TEXT, T_AUDIO = (4, 512, 375)
        s = 0.02
        return {'hidden_states': jax.random.normal(ks[0], (B, T_TEXT, HIDDEN), jnp.float32), 'audio_kv': jax.random.normal(ks[1], (B, T_AUDIO, HIDDEN), jnp.float32), 'audio_attention_mask': jnp.ones((B, T_AUDIO), dtype=bool), 'Wq': jax.random.normal(ks[2], (HIDDEN, HIDDEN), jnp.float32) * s, 'Wk': jax.random.normal(ks[3], (HIDDEN, HIDDEN), jnp.float32) * s, 'Wv': jax.random.normal(ks[4], (HIDDEN, HIDDEN), jnp.float32) * s, 'Wo': jax.random.normal(ks[5], (HIDDEN, HIDDEN), jnp.float32) * s, 'ln_gamma': jnp.ones((HIDDEN,), jnp.float32), 'ln_beta': jnp.zeros((HIDDEN,), jnp.float32), 'gate': jnp.array([GATE_INIT], jnp.float32)}
    _L1_xattn_all = _L1_xattn_setup()
    _L1_xattn_in = {k: v for k, v in _L1_xattn_all.items() if k in ('Wq', 'Wk', 'Wv', 'Wo', 'ln_gamma', 'ln_beta', 'gate')}
    del _L1_xattn_all

    def _L2_xattn_setup():
        import jax, jax.numpy as jnp
        import numpy as np
        D = 512
        H = 16
        HD = D // H
        INNER = 4 * D
        EPS = 1e-05

        def layer_norm(x, w, b):
            mu = jnp.mean(x, axis=-1, keepdims=True)
            var = jnp.mean(jnp.square(x - mu), axis=-1, keepdims=True)
            return (x - mu) * jax.lax.rsqrt(var + EPS) * w + b
        key = jax.random.key(seed)
        ks = jax.random.split(key, 12)
        B, LQ, LK = (4, 256, 512)
        std = 0.02
        inp = {'hidden_states': jax.random.normal(ks[0], (B, LQ, D), jnp.float32), 'encoder_hidden_states': jax.random.normal(ks[1], (B, LK, D), jnp.float32), 'encoder_attention_mask': jnp.ones((B, LK), dtype=bool), 'ln1_w': jnp.ones((D,), jnp.float32), 'ln1_b': jnp.zeros((D,), jnp.float32), 'q_w': jax.random.normal(ks[2], (D, D), jnp.float32) * std, 'q_b': jnp.zeros((D,), jnp.float32), 'k_w': jax.random.normal(ks[3], (D, D), jnp.float32) * std, 'k_b': jnp.zeros((D,), jnp.float32), 'v_w': jax.random.normal(ks[4], (D, D), jnp.float32) * std, 'v_b': jnp.zeros((D,), jnp.float32), 'cproj_w': jax.random.normal(ks[5], (D, D), jnp.float32) * std, 'cproj_b': jnp.zeros((D,), jnp.float32), 'ln2_w': jnp.ones((D,), jnp.float32), 'ln2_b': jnp.zeros((D,), jnp.float32), 'fc_w': jax.random.normal(ks[6], (D, INNER), jnp.float32) * std, 'fc_b': jnp.zeros((INNER,), jnp.float32), 'proj_w': jax.random.normal(ks[7], (INNER, D), jnp.float32) * std, 'proj_b': jnp.zeros((D,), jnp.float32)}
        return inp
    _L2_xattn_all = _L2_xattn_setup()
    _L2_xattn_in = {k: v for k, v in _L2_xattn_all.items() if k in ('ln1_w', 'ln1_b', 'q_w', 'q_b', 'k_w', 'k_b', 'v_w', 'v_b', 'cproj_w', 'cproj_b', 'ln2_w', 'ln2_b', 'fc_w', 'fc_b', 'proj_w', 'proj_b')}
    del _L2_xattn_all

    def _L3_xattn_setup():
        import jax, jax.numpy as jnp
        import numpy as np
        H = 512
        NH = 32
        KVH = 8
        HD = H // NH
        GROUPS = NH // KVH
        EPS = 1e-06
        B, L, S = (4, 256, 256)

        def _gqa_forward(hidden_state, encoder_hidden_state, encoder_attention_mask, Wq, bq, Wk, bk, Wv, bv, Wo, bo, gamma, beta):
            b, l, _ = hidden_state.shape
            s = encoder_hidden_state.shape[1]
            q = hidden_state @ Wq + bq
            k = encoder_hidden_state @ Wk + bk
            v = encoder_hidden_state @ Wv + bv
            q = q.reshape(b, l, KVH, GROUPS, HD).transpose(0, 2, 3, 1, 4)
            k = k.reshape(b, s, KVH, HD).transpose(0, 2, 1, 3)
            v = v.reshape(b, s, KVH, HD).transpose(0, 2, 1, 3)
            scale = 1.0 / jnp.sqrt(jnp.asarray(HD, q.dtype))
            scores = jnp.einsum('bkgld,bksd->bkgls', q, k) * scale
            scores = scores + encoder_attention_mask[:, :, None, :, :]
            attn = jax.nn.softmax(scores, axis=-1)
            out = jnp.einsum('bkgls,bksd->bkgld', attn, v)
            out = out.transpose(0, 3, 1, 2, 4).reshape(b, l, H)
            out = out @ Wo + bo
            x = out + hidden_state
            mu = jnp.mean(x, axis=-1, keepdims=True)
            var = jnp.var(x, axis=-1, keepdims=True)
            return (x - mu) * jax.lax.rsqrt(var + EPS) * gamma + beta
        key = jax.random.key(seed)
        ks = jax.random.split(key, 12)
        sd = 0.02
        return {'hidden_state': jax.random.normal(ks[0], (B, L, H), jnp.float32), 'encoder_hidden_state': jax.random.normal(ks[1], (B, S, H), jnp.float32), 'encoder_attention_mask': jnp.zeros((B, 1, L, S), jnp.float32), 'Wq': jax.random.normal(ks[2], (H, H), jnp.float32) * sd, 'bq': jnp.zeros((H,), jnp.float32), 'Wk': jax.random.normal(ks[3], (H, KVH * HD), jnp.float32) * sd, 'bk': jnp.zeros((KVH * HD,), jnp.float32), 'Wv': jax.random.normal(ks[4], (H, KVH * HD), jnp.float32) * sd, 'bv': jnp.zeros((KVH * HD,), jnp.float32), 'Wo': jax.random.normal(ks[5], (H, H), jnp.float32) * sd, 'bo': jnp.zeros((H,), jnp.float32), 'gamma': jnp.ones((H,), jnp.float32), 'beta': jnp.zeros((H,), jnp.float32)}
    _L3_xattn_all = _L3_xattn_setup()
    _L3_xattn_in = {k: v for k, v in _L3_xattn_all.items() if k in ('Wq', 'bq', 'Wk', 'bk', 'Wv', 'bv', 'Wo', 'bo', 'gamma', 'beta')}
    del _L3_xattn_all
    return {'x': x, 'ctx_2048': ctx_2048, 'mask_Bx1x2048_bf1': mask_Bx1x2048_bf1, 'mask_BxS2_bf1': mask_BxS2_bf1, 'mask_Bx1xSxS2_ff0': mask_Bx1xSxS2_ff0, 'L0_xattn_Wq': _L0_xattn_in['Wq'], 'L0_xattn_bq': _L0_xattn_in['bq'], 'L0_xattn_Wk': _L0_xattn_in['Wk'], 'L0_xattn_bk': _L0_xattn_in['bk'], 'L0_xattn_Wv': _L0_xattn_in['Wv'], 'L0_xattn_bv': _L0_xattn_in['bv'], 'L1_xattn_Wq': _L1_xattn_in['Wq'], 'L1_xattn_Wk': _L1_xattn_in['Wk'], 'L1_xattn_Wv': _L1_xattn_in['Wv'], 'L1_xattn_Wo': _L1_xattn_in['Wo'], 'L1_xattn_ln_gamma': _L1_xattn_in['ln_gamma'], 'L1_xattn_ln_beta': _L1_xattn_in['ln_beta'], 'L1_xattn_gate': _L1_xattn_in['gate'], 'L2_xattn_ln1_w': _L2_xattn_in['ln1_w'], 'L2_xattn_ln1_b': _L2_xattn_in['ln1_b'], 'L2_xattn_q_w': _L2_xattn_in['q_w'], 'L2_xattn_q_b': _L2_xattn_in['q_b'], 'L2_xattn_k_w': _L2_xattn_in['k_w'], 'L2_xattn_k_b': _L2_xattn_in['k_b'], 'L2_xattn_v_w': _L2_xattn_in['v_w'], 'L2_xattn_v_b': _L2_xattn_in['v_b'], 'L2_xattn_cproj_w': _L2_xattn_in['cproj_w'], 'L2_xattn_cproj_b': _L2_xattn_in['cproj_b'], 'L2_xattn_ln2_w': _L2_xattn_in['ln2_w'], 'L2_xattn_ln2_b': _L2_xattn_in['ln2_b'], 'L2_xattn_fc_w': _L2_xattn_in['fc_w'], 'L2_xattn_fc_b': _L2_xattn_in['fc_b'], 'L2_xattn_proj_w': _L2_xattn_in['proj_w'], 'L2_xattn_proj_b': _L2_xattn_in['proj_b'], 'L3_xattn_Wq': _L3_xattn_in['Wq'], 'L3_xattn_bq': _L3_xattn_in['bq'], 'L3_xattn_Wk': _L3_xattn_in['Wk'], 'L3_xattn_bk': _L3_xattn_in['bk'], 'L3_xattn_Wv': _L3_xattn_in['Wv'], 'L3_xattn_bv': _L3_xattn_in['bv'], 'L3_xattn_Wo': _L3_xattn_in['Wo'], 'L3_xattn_bo': _L3_xattn_in['bo'], 'L3_xattn_gamma': _L3_xattn_in['gamma'], 'L3_xattn_beta': _L3_xattn_in['beta']}

def reference(x, ctx_2048, mask_Bx1x2048_bf1, mask_BxS2_bf1, mask_Bx1xSxS2_ff0, L0_xattn_Wq, L0_xattn_bq, L0_xattn_Wk, L0_xattn_bk, L0_xattn_Wv, L0_xattn_bv, L1_xattn_Wq, L1_xattn_Wk, L1_xattn_Wv, L1_xattn_Wo, L1_xattn_ln_gamma, L1_xattn_ln_beta, L1_xattn_gate, L2_xattn_ln1_w, L2_xattn_ln1_b, L2_xattn_q_w, L2_xattn_q_b, L2_xattn_k_w, L2_xattn_k_b, L2_xattn_v_w, L2_xattn_v_b, L2_xattn_cproj_w, L2_xattn_cproj_b, L2_xattn_ln2_w, L2_xattn_ln2_b, L2_xattn_fc_w, L2_xattn_fc_b, L2_xattn_proj_w, L2_xattn_proj_b, L3_xattn_Wq, L3_xattn_bq, L3_xattn_Wk, L3_xattn_bk, L3_xattn_Wv, L3_xattn_bv, L3_xattn_Wo, L3_xattn_bo, L3_xattn_gamma, L3_xattn_beta):
    import jax
    import jax.numpy as jnp

    def _L0_xattn_ref(x, mask, kv, kv_mask, Wq, bq, Wk, bk, Wv, bv):
        import jax, jax.numpy as jnp
        import numpy as np
        import math
        N_HEADS = 16
        EPS = 1e-05

        def _masked_instance_norm(x, mask):
            m = mask.astype(x.dtype)
            x = x * m
            n_valid = jnp.sum(m, axis=-1, keepdims=True)
            mean = jnp.sum(x, axis=-1, keepdims=True) / n_valid
            var = jnp.sum(x * x, axis=-1, keepdims=True) / n_valid - mean * mean
            x = (x - mean) / jnp.sqrt(jax.nn.relu(var) + EPS)
            return x * m
        bs, c, t1 = x.shape
        h = N_HEADS
        d = c // h
        scale = 1.0 / math.sqrt(d)
        q = jnp.einsum('oc,bct->bot', Wq, x) + bq[None, :, None]
        k = jnp.einsum('oc,bct->bot', Wk, kv) + bk[None, :, None]
        v = jnp.einsum('oc,bct->bot', Wv, kv) + bv[None, :, None]
        q = q.reshape(bs, h, d, t1).transpose(0, 1, 3, 2)
        k = k.reshape(bs, h, d, -1)
        v = v.reshape(bs, h, d, -1).transpose(0, 1, 3, 2)
        attn = jnp.einsum('bhqd,bhdk->bhqk', q * scale, k)
        attn = jnp.where(kv_mask[:, :, None, :], attn, -jnp.inf)
        attn = jax.nn.softmax(attn, axis=-1)
        mean = jnp.einsum('bhqk,bhkd->bhqd', attn, v)
        ex2 = jnp.einsum('bhqk,bhkd->bhqd', attn, v * v)
        std = jnp.sqrt(jax.nn.relu(ex2 - mean * mean))
        mean = mean.transpose(0, 1, 3, 2).reshape(bs, c, t1)
        std = std.transpose(0, 1, 3, 2).reshape(bs, c, t1)
        xn = _masked_instance_norm(x, mask)
        out = (xn * std + mean) * mask.astype(x.dtype)
        return out

    def _L1_xattn_ref(hidden_states, audio_kv, audio_attention_mask, Wq, Wk, Wv, Wo, ln_gamma, ln_beta, gate):
        import jax, jax.numpy as jnp
        import numpy as np
        HIDDEN = 512
        HEADS = 16
        HEAD_DIM = HIDDEN // HEADS
        LN_EPS = 1e-05
        GATE_INIT = 0.5

        def _layer_norm(x, gamma, beta):
            mu = jnp.mean(x, axis=-1, keepdims=True)
            var = jnp.mean(jnp.square(x - mu), axis=-1, keepdims=True)
            return (x - mu) * jax.lax.rsqrt(var + LN_EPS) * gamma + beta
        B, Tt, D = hidden_states.shape
        Ta = audio_kv.shape[1]
        scale = HEAD_DIM ** (-0.5)
        a = _layer_norm(audio_kv, ln_gamma, ln_beta)
        Q = (hidden_states @ Wq.T).reshape(B, Tt, HEADS, HEAD_DIM).transpose(0, 2, 1, 3)
        K = (a @ Wk.T).reshape(B, Ta, HEADS, HEAD_DIM).transpose(0, 2, 1, 3)
        V = (a @ Wv.T).reshape(B, Ta, HEADS, HEAD_DIM).transpose(0, 2, 1, 3)
        scores = jnp.einsum('bhtd,bhsd->bhts', Q, K) * scale
        mask = audio_attention_mask[:, None, None, :]
        scores = jnp.where(mask, scores, jnp.float32(-jnp.inf))
        attn = jax.nn.softmax(scores, axis=-1)
        out = jnp.einsum('bhts,bhsd->bhtd', attn, V)
        out = out.transpose(0, 2, 1, 3).reshape(B, Tt, D)
        out = out @ Wo.T
        return hidden_states + jnp.tanh(gate) * out

    def _L2_xattn_ref(hidden_states, encoder_hidden_states, encoder_attention_mask, ln1_w, ln1_b, q_w, q_b, k_w, k_b, v_w, v_b, cproj_w, cproj_b, ln2_w, ln2_b, fc_w, fc_b, proj_w, proj_b):
        import jax, jax.numpy as jnp
        import numpy as np
        D = 512
        H = 16
        HD = D // H
        INNER = 4 * D
        EPS = 1e-05

        def layer_norm(x, w, b):
            mu = jnp.mean(x, axis=-1, keepdims=True)
            var = jnp.mean(jnp.square(x - mu), axis=-1, keepdims=True)
            return (x - mu) * jax.lax.rsqrt(var + EPS) * w + b
        B, LQ, _ = hidden_states.shape
        LK = encoder_hidden_states.shape[1]
        residual = hidden_states
        x = layer_norm(hidden_states, ln1_w, ln1_b)
        q = (x @ q_w + q_b).reshape(B, LQ, H, HD).transpose(0, 2, 1, 3)
        k = (encoder_hidden_states @ k_w + k_b).reshape(B, LK, H, HD).transpose(0, 2, 1, 3)
        v = (encoder_hidden_states @ v_w + v_b).reshape(B, LK, H, HD).transpose(0, 2, 1, 3)
        scale = 1.0 / np.sqrt(HD).astype(np.float32)
        scores = jnp.einsum('bhqd,bhkd->bhqk', q, k) * scale
        mask = encoder_attention_mask[:, None, None, :]
        mask_value = jnp.finfo(scores.dtype).min
        scores = jnp.where(mask, scores, mask_value)
        attn = jax.nn.softmax(scores, axis=-1)
        out = jnp.einsum('bhqk,bhkd->bhqd', attn, v)
        out = out.transpose(0, 2, 1, 3).reshape(B, LQ, D)
        out = out @ cproj_w + cproj_b
        hidden = out + residual
        residual = hidden
        y = layer_norm(hidden, ln2_w, ln2_b)
        y = jax.nn.gelu(y @ fc_w + fc_b, approximate=True)
        y = y @ proj_w + proj_b
        return residual + y

    def _L3_xattn_ref(hidden_state, encoder_hidden_state, encoder_attention_mask, Wq, bq, Wk, bk, Wv, bv, Wo, bo, gamma, beta):
        import jax, jax.numpy as jnp
        import numpy as np
        H = 512
        NH = 32
        KVH = 8
        HD = H // NH
        GROUPS = NH // KVH
        EPS = 1e-06
        B, L, S = (4, 256, 256)

        def _gqa_forward(hidden_state, encoder_hidden_state, encoder_attention_mask, Wq, bq, Wk, bk, Wv, bv, Wo, bo, gamma, beta):
            b, l, _ = hidden_state.shape
            s = encoder_hidden_state.shape[1]
            q = hidden_state @ Wq + bq
            k = encoder_hidden_state @ Wk + bk
            v = encoder_hidden_state @ Wv + bv
            q = q.reshape(b, l, KVH, GROUPS, HD).transpose(0, 2, 3, 1, 4)
            k = k.reshape(b, s, KVH, HD).transpose(0, 2, 1, 3)
            v = v.reshape(b, s, KVH, HD).transpose(0, 2, 1, 3)
            scale = 1.0 / jnp.sqrt(jnp.asarray(HD, q.dtype))
            scores = jnp.einsum('bkgld,bksd->bkgls', q, k) * scale
            scores = scores + encoder_attention_mask[:, :, None, :, :]
            attn = jax.nn.softmax(scores, axis=-1)
            out = jnp.einsum('bkgls,bksd->bkgld', attn, v)
            out = out.transpose(0, 3, 1, 2, 4).reshape(b, l, H)
            out = out @ Wo + bo
            x = out + hidden_state
            mu = jnp.mean(x, axis=-1, keepdims=True)
            var = jnp.var(x, axis=-1, keepdims=True)
            return (x - mu) * jax.lax.rsqrt(var + EPS) * gamma + beta
        return _gqa_forward(hidden_state, encoder_hidden_state, encoder_attention_mask, Wq, bq, Wk, bk, Wv, bv, Wo, bo, gamma, beta)
    x = _L0_xattn_ref(x, mask_Bx1x2048_bf1, ctx_2048, mask_Bx1x2048_bf1, L0_xattn_Wq, L0_xattn_bq, L0_xattn_Wk, L0_xattn_bk, L0_xattn_Wv, L0_xattn_bv)
    x = _L1_xattn_ref(x, ctx_2048, mask_BxS2_bf1, L1_xattn_Wq, L1_xattn_Wk, L1_xattn_Wv, L1_xattn_Wo, L1_xattn_ln_gamma, L1_xattn_ln_beta, L1_xattn_gate)
    x = _L2_xattn_ref(x, ctx_2048, mask_BxS2_bf1, L2_xattn_ln1_w, L2_xattn_ln1_b, L2_xattn_q_w, L2_xattn_q_b, L2_xattn_k_w, L2_xattn_k_b, L2_xattn_v_w, L2_xattn_v_b, L2_xattn_cproj_w, L2_xattn_cproj_b, L2_xattn_ln2_w, L2_xattn_ln2_b, L2_xattn_fc_w, L2_xattn_fc_b, L2_xattn_proj_w, L2_xattn_proj_b)
    x = _L3_xattn_ref(x, ctx_2048, mask_Bx1xSxS2_ff0, L3_xattn_Wq, L3_xattn_bq, L3_xattn_Wk, L3_xattn_bk, L3_xattn_Wv, L3_xattn_bv, L3_xattn_Wo, L3_xattn_bo, L3_xattn_gamma, L3_xattn_beta)
    return x

_drawn_inputs = setup_inputs


def setup_inputs(seed=0):
    import zlib

    import numpy as np

    out = dict(_drawn_inputs(seed))
    spreads = {'L0_xattn_bq': (0.0, 0.8),
     'L0_xattn_bk': (0.0, 0.8),
     'L0_xattn_bv': (0.0, 0.8),
     'L1_xattn_ln_gamma': (1.0, 0.6),
     'L1_xattn_ln_beta': (0.0, 0.8),
     'L2_xattn_ln1_w': (1.0, 0.6),
     'L2_xattn_ln1_b': (0.0, 0.8),
     'L2_xattn_q_b': (0.0, 0.8),
     'L2_xattn_k_b': (0.0, 0.8),
     'L2_xattn_v_b': (0.0, 0.1),
     'L2_xattn_cproj_b': (0.0, 0.1),
     'L2_xattn_ln2_w': (1.0, 0.2),
     'L2_xattn_ln2_b': (0.0, 0.322),
     'L2_xattn_fc_b': (0.0, 0.1),
     'L2_xattn_proj_b': (0.0, 0.1),
     'L3_xattn_bq': (0.0, 0.8),
     'L3_xattn_bk': (0.0, 0.8),
     'L3_xattn_bv': (0.0, 0.1),
     'L3_xattn_bo': (0.0, 0.1),
     'L3_xattn_gamma': (1.0, 0.2),
     'L3_xattn_beta': (0.0, 0.1)}
    factors = {'L1_xattn_Wq': 8.0,
     'L1_xattn_Wk': 8.0,
     'L2_xattn_q_w': 7.17,
     'L2_xattn_k_w': 7.006,
     'L3_xattn_Wq': 7.584,
     'L3_xattn_Wk': 7.389}
    for name, (base, spread) in spreads.items():
        noise = np.random.default_rng([zlib.crc32(name.encode()), seed]).standard_normal(out[name].shape)
        drawn = base * np.exp(spread * noise) if base else spread * noise
        out[name] = jnp.asarray(drawn.astype(out[name].dtype))
    for name, factor in factors.items():
        out[name] = (out[name] * factor).astype(out[name].dtype)
    return out
```

```python
import numpy as np
from contextlib import ExitStack
import concourse.bass as bass
import concourse.mybir as mybir

F32 = mybir.dt.float32
F32R = mybir.dt.float32r
U8 = mybir.dt.uint8
ALU = mybir.AluOpType
ACT = mybir.ActivationFunctionType
AX = mybir.AxisListType

P = 128
TOK = 256
DM = 512
WIN = 256
BANK = 512
STACK = 96
ROW1 = 96
NEG = -1.0e30
INNER = 2048
HI, LO = 0, 1


class Layer:

    def __init__(self, name, keys, steps, heads, tiles, rows, dv, kv_heads, q_tiles, q_width, scale):
        self.name = name
        self.keys = keys
        self.kt = keys // P
        self.steps = steps
        self.heads = heads
        self.tiles = tiles
        self.rows = rows
        self.mtiles = 2 if name == 3 else 1
        self.depth = ROW1 + 1 + rows
        self.dv = dv
        self.kv_heads = kv_heads
        self.q_tiles = q_tiles
        self.q_width = q_width
        self.scale = scale


L0 = Layer(0, DM, 16, 2, 1, 2, 32, 16, 8, DM, 0.25)
L1 = Layer(1, TOK, 4, 4, 4, 4, 32, 16, 16, TOK, 32 ** -0.5)
L2 = Layer(2, TOK, 4, 4, 4, 4, 32, 16, 16, TOK, 32 ** -0.5)
L3 = Layer(3, TOK, 8, 4, 2, 2, 16, 8, 16, TOK, 1.0)


def words(ap):
    return ap.bitcast(F32)


def wait(eng, sem, value):
    if isinstance(value, int) and value <= 0:
        return
    eng.wait_ge(sem, value)


def wait_apart(eng, sem, value, passed):
    wait(eng, sem, value)
    if not isinstance(value, int):
        eng.sem_inc(passed, 1)


def give_back(nc, used):
    with nc.Block() as block:
        @block.sync
        def _(sp):
            for s in used[0::3]:
                sp.sem_clear(s)

        @block.scalar
        def _(act):
            for s in used[1::3]:
                act.sem_clear(s)

        @block.vector
        def _(dve):
            for s in used[2::3]:
                dve.sem_clear(s)


def split_weights(nc, sem, weights, stage):
    slots = stage.shape[1]
    chunks = [(src[:, c, :], dst[:, HI, c, :], dst[:, LO, c, :], src.shape[2])
              for src, dst in weights for c in range(src.shape[1])]
    raw = [sem(f"wraw{i}") for i in range(slots)]
    hi_done = sem("whi")
    lo_done = sem("wlo")
    with nc.Block() as block:
        @block.sync
        def _(sp):
            for n, (src, _, _, w) in enumerate(chunks):
                wait(sp, lo_done, n - slots + 1)
                sp.dma_start(stage[:, n % slots, 0:w], src).then_inc(raw[n % slots], 16)
            sp.wait_ge(lo_done, len(chunks))

        @block.scalar
        def _(act):
            for n, (_, hi, _, w) in enumerate(chunks):
                act.wait_ge(raw[n % slots], 16 * (n // slots + 1))
                act.activation(hi, stage[:, n % slots, 0:w], ACT.Copy).then_inc(hi_done, 1)

        @block.vector
        def _(dve):
            for n, (_, hi, lo, w) in enumerate(chunks):
                dve.wait_ge(hi_done, n + 1)
                dve.tensor_tensor(lo, stage[:, n % slots, 0:w], hi.bitcast(F32),
                                  ALU.subtract).then_inc(lo_done, 1)


def exact_product(pe, out, lhs, rhs, depth, start=True, stop=True):
    last = None
    for k in range(depth):
        for n, (a, b) in enumerate(((HI, HI), (HI, LO), (LO, HI))):
            last = pe.matmul(out, lhs(k, a), rhs(k, b), start=start and k == 0 and n == 0,
                             stop=stop and k == depth - 1 and n == 2)
    return last


def attention_layer(nc, L, NB, D, x_in, ctx_in, out):
    name = L.name
    NS = L.steps
    UB = 5 * NS
    heads_jobs = {0: ["Q0", "V0", "Q1", "V1", "K0", "K1"],
                  1: ["XT0", "XT1", "CT0", "CT1", "Q0", "Q1", "K0", "K1", "V0", "V1"],
                  2: ["XT0", "XT1", "Q0", "Q1", "K0", "K1", "V0", "V1"],
                  3: ["XT0", "XT1", "Q0", "Q1", "K0", "V0"]}[name]
    tail_jobs = ["STD0", "MEAN0", "STD1", "MEAN1"] if name == 0 else ["AT0", "AT1", "O0", "O1"]
    NH, NT = len(heads_jobs), len(tail_jobs)
    NJ = NH + NT
    split_head = [j for j in heads_jobs if j[0] != "V"]
    split_tail = [] if name == 0 else ["AT0", "AT1"]
    SH, SJ = len(split_head), len(split_head) + len(split_tail)

    with ExitStack() as ctx:
        def sb(n, shape, dt):
            return ctx.enter_context(nc.sbuf_tensor(f"l{name}_{n}", shape, dt))

        used = []

        def sem(n):
            used.append(ctx.enter_context(nc.semaphore(f"l{name}_{n}")))
            return used[-1]

        QS = sb("query_stack", [P, 2, L.q_tiles, L.q_width], F32R)
        KS = sb("key_stack", [P, 2, L.kv_heads, L.keys], F32R)
        V = sb("values", [P, 2, L.kt, L.kv_heads, L.dv + 1], F32)
        PR = sb("probs", [P, 2, 4, BANK], F32)
        AO = sb("attended", [P, 2 * L.q_width // 256, DM] if name else [P, 4, 2 * TOK], F32)
        NAT = sb("natural", [P, 2, 2, BANK], F32R)
        TMP = sb("evacuated", [P, 2, BANK], F32)
        XF = sb("x_raw", [P, 2, DM], F32)
        CF = sb("ctx_raw", [P, 2, DM], F32)
        XR = sb("x_residual", [P, 2, DM], F32)
        NM = sb("minus_max", [P, 2, L.mtiles, 2, L.depth], F32R)
        RC = sb("reciprocals", [P, 2 * L.heads], F32)
        IDF = sb("ident", [P, P], F32)
        IDR = sb("ident_r", [P, P], F32R)
        CONST = sb("constants", [P, 2], F32)
        OHF = sb("onehot_f", [P, L.rows], F32)
        OHR = NAT[:, :, :, :].rearrange("p s h n -> p (s h n)")[:, 0:L.rows * L.keys].rearrange(
            "p (r n) -> p r n", r=L.rows)
        if name == 0:
            XS = sb("x_split", [P, 2, 2, DM], F32R)
            CS = sb("ctx_split", [P, 2, 2, DM], F32R)
        else:
            XS = sb("x_split", [P, 2, 4, TOK], F32R)
            CS = sb("ctx_split", [P, 2, 4, TOK], F32R)
        kin = 2 if name == 0 else 4
        wq_n = TOK if name == 0 else DM
        wk_n = {0: TOK, 3: P}.get(name, DM)
        WQ = sb("wq", [P, 2, kin, wq_n], F32R)
        WK = sb("wk", [P, 2, kin, wk_n], F32R)
        WV = sb("wv", [P, 2, kin, wk_n], F32R)
        weights = [(D["wq"].rearrange("(k p) n -> p k n", p=P), WQ),
                   (D["wk"].rearrange("(k p) n -> p k n", p=P), WK),
                   (D["wv"].rearrange("(k p) n -> p k n", p=P), WV)]
        if name:
            WO = sb("wo", [P, 2, 4, DM], F32R)
            weights.append((D["wo"].rearrange("(k p) n -> p k n", p=P), WO))
        if name != 1:
            BQ = sb("bq", [P, wq_n // P], F32)
            BK = sb("bk", [P, max(wk_n // P, 1)], F32)
            BV = sb("bv", [P, wk_n], F32)
        if name != 3:
            MU8 = sb("mask_bytes", [P, L.keys], U8)
            MRF = sb("mask_row_f", [P, L.keys], F32) if name != 2 else None
            MRR = sb("mask_row", [P, L.keys], F32R)
        if name == 0:
            QM8 = sb("query_mask_bytes", [P, DM], U8)
            QM = sb("query_mask", [P, DM], F32)
            SQ = sb("squares", [P, DM], F32)
            ST8 = sb("x_stats", [P, 10], F32)
        if name in (1, 2):
            G1 = sb("norm_w", [P, 4], F32)
            B1 = sb("norm_b", [P, 4], F32)
            BN = sb("bn", [P, 2, 6], F32)
            MV = sb("mean_var", [P, 2, 2], F32)
            RS = sb("rstd", [P, 2], F32)
        if name == 1:
            GT = sb("gate", [P, 1], F32)
        if name in (2, 3):
            BO = sb("out_bias", [P, DM], F32)
        if name == 3:
            MKF = sb("mask_raw", [P, 2, 2, TOK], F32)
            MKC = sb("mask_clamped", [P, 2, 2, TOK], F32)
            MKS = sb("mask_split", [P, 2, 2, 2, 2, TOK], F32R)
            GA = sb("gamma", [P, DM], F32)
            BE = sb("beta", [P, DM], F32)
            BN = sb("bn", [P, 2, 6], F32)
            MV = sb("mean_var", [P, 2, 2], F32)
            RS = sb("rstd", [P, 2], F32)

        SB = ctx.enter_context(nc.psum_tensor(f"l{name}_scores", [P, 2, BANK], F32))
        AB = ctx.enter_context(nc.psum_tensor(f"l{name}_scores_t", [P, 2, BANK], F32))
        OB = ctx.enter_context(nc.psum_tensor(f"l{name}_out", [P, 2, BANK], F32))
        FB = ctx.enter_context(nc.psum_tensor(f"l{name}_jobs", [P, 2, BANK], F32))

        c_ident = sem("c_ident")
        c_load = sem("c_load")
        c_set = sem("c_set")
        c_onehot = sem("c_onehot")
        c_pool = sem("c_pool")
        consts = []
        if name != 1:
            consts += [(BQ[:, :], D["bq"]), (BK[:, :], D["bk"]),
                       (BV[:, :], D["bv"].partition_broadcast(P))]
        if name in (1, 2):
            consts += [(G1[:, :], D["ln_w"]), (B1[:, :], D["ln_b"])]
        if name == 1:
            consts += [(GT[:, :], D["gate"].partition_broadcast(P))]
        if name in (2, 3):
            consts += [(BO[:, :], D["bo"].partition_broadcast(P))]
        if name == 3:
            consts += [(GA[:, :], D["gamma"].partition_broadcast(P)),
                       (BE[:, :], D["beta"].partition_broadcast(P))]
        with nc.Block() as block:
            @block.gpsimd
            def _(pool):
                pool.memset(IDF[:, :], 0.0).then_inc(c_pool, 1)
                pool.memset(OHF[:, :], 0.0).then_inc(c_pool, 1)
                for n, value in enumerate((-0.5, 1e-6 if name == 3 else 1e-5)):
                    pool.memset(CONST[:, n:n + 1], value).then_inc(c_pool, 1)
                pool.wait_ge(c_pool, 2)
                pool.affine_select(out=IDF[:, :], in_=IDF[:, :], compare_op=ALU.not_equal, fill=1.0,
                                   base=0, pattern=[[-1, P]], channel_multiplier=1).then_inc(c_ident, 1)
                pool.affine_select(out=OHF[:, :], in_=OHF[:, :], compare_op=ALU.not_equal, fill=1.0,
                                   base=-(ROW1 + 1), pattern=[[-1, L.rows]], channel_multiplier=1).then_inc(c_ident, 1)
                pool.memset(V[:, :, :, :, L.dv:L.dv + 1], 1.0).then_inc(c_pool, 1)

            @block.vector
            def _(dve):
                dve.memset(NM[:, :, :, :, :].bitcast(F32), 0.0).then_inc(c_set, 1)
                dve.memset(QS[ROW1:L.depth, :, :, :].bitcast(F32), 1.0).then_inc(c_set, 1)
                if name in (0, 3):
                    dve.memset(KS[0:STACK, :, :, :].bitcast(F32), 0.0).then_inc(c_set, 1)
                dve.wait_ge(c_set, 1)
                dve.memset(NM[:, :, :, :, ROW1:ROW1 + 1].bitcast(F32), 1.0).then_inc(c_set, 1)
                dve.wait_ge(c_ident, 2)
                dve.tensor_copy(IDR[:, :], IDF[:, :]).then_inc(c_set, 1)
                for r in range(L.rows):
                    src = OHF[ROW1:L.depth, r:r + 1].to_broadcast([L.rows + 1, L.keys])
                    dve.tensor_copy(OHR[ROW1:L.depth, r, :], src).then_inc(c_onehot, 1)

            @block.sync
            def _(sp):
                for dst, src in consts:
                    sp.dma_start(dst, src).then_inc(c_load, 16)
                sp.wait_ge(c_onehot, L.rows)
                for par in range(2):
                    for r in range(L.rows):
                        sp.dma_start(
                            words(KS[ROW1:L.depth, par, r:L.kv_heads:L.rows, :]),
                            words(OHR[ROW1:L.depth, r:r + 1, :]).to_broadcast(
                                [L.rows + 1, L.kv_heads // L.rows, L.keys])).then_inc(c_load, 16)
                sp.wait_ge(c_load, 16 * (len(consts) + 2 * L.rows))

            if name == 1:
                @block.scalar
                def _(act):
                    act.wait_ge(c_load, 16 * (len(consts) + 2 * L.rows))
                    act.activation(GT[:, :], GT[:, :], ACT.Tanh).then_inc(c_set, 1)

        split_weights(nc, sem, weights, PR[:, :, :, :].rearrange("p a b n -> p (a b) n"))

        scores_ready = sem("scores_ready")
        maxima_done = sem("maxima_done")
        act_ready = sem("act_ready")
        act_done = sem("act_done")
        av_done = sem("av_done")
        recip_done = sem("recip_done")
        norm_done = sem("norm_done")
        job_ready = sem("job_ready")
        bank_free = [sem("bank_free0"), sem("bank_free1")]
        hi_done = sem("hi_done")
        lo_done = sem("lo_done")
        nat_moved = [sem("nat_moved0"), sem("nat_moved1")]
        in_x, in_c, in_r, in_m = sem("in_x"), sem("in_c"), sem("in_r"), sem("in_m")
        x_hi = sem("x_hi")
        x_lo = sem("x_lo")
        y_stored = sem("y_stored")
        sp_passed, dve_passed = sem("sp_passed"), sem("dve_passed")
        if name == 0:
            v_mid = sem("v_mid")
            v_ready = sem("v_ready")
            qmask_done = sem("qmask_done")
            masked_done = sem("masked_done")
            sums_done = sem("sums_done")
            xn_done = sem("xn_done")
            xrstd_done = sem("xrstd_done")
            dev_done = sem("dev_done")
            root_done = sem("root_done")
            y_ready = sem("y_ready")
        if name in (1, 2):
            ln_done = sem("ln_done")
            rstd_done = sem("rstd_done")
        if name == 2:
            res_biased = sem("res_biased")
        if name == 3:
            m_clamped = sem("m_clamped")
            m_hi = sem("m_hi")
            m_lo = sem("m_lo")
            res_biased = sem("res_biased")
            ln_done = sem("ln_done")
            rstd_done = sem("rstd_done")
        else:
            m_row = sem("m_row")
            m_moved = [sem("m_moved0"), sem("m_moved1")]

        split_index = {j: n for n, j in enumerate(split_head + split_tail)}
        nat_slot = {j: n % 2 for n, j in enumerate(x for x in heads_jobs if x[0] in "QK")}
        moves = {j: (24 if j[0] == "K" and name in (0, 3) else 12) for j in nat_slot}
        per_head = [sum(moves[j] for j in nat_slot if nat_slot[j] == n) for n in range(2)]
        V_JOBS = 2 if name == 0 else 0

        def moved(job, e):
            n, seen = nat_slot[job], 0
            for j in nat_slot:
                if j == job:
                    break
                seen += moves[j] if nat_slot[j] == n else 0
            return 16 * (per_head[n] * e + seen)

        def unit(b, s, k):
            if k < 0:
                return UB * b + (0 if s == 0 else 5 * s - 2)
            return UB * b + 1 + 5 * s + (k + 1 if k >= 2 and s < NS - 1 else k)

        def stacks_of(s, j):
            if name == 0:
                return s // 2, (s % 2) * WIN, 2 * (s // 2) + j // 2
            if name == 3:
                return 2 * s + j // 2, 0, 2 * (s // 2) + j % 2
            return 4 * s + j, 0, 4 * s + j

        def count_before(jbase, k):
            return jbase // 2 + k // 2 if isinstance(jbase, int) else jbase[1] + k // 2

        def J(jbase):
            return jbase if isinstance(jbase, int) else jbase[0]

        def pe_scores(pe, b, par, s, j):
            qt, q0, kh = stacks_of(s, j)
            wait(pe, maxima_done, 4 * (NS * b + s) + j - 1)
            bank = SB[:, j % 2, :]
            last = None
            if name == 0:
                c = q0 + (j % 2) * P
                last = pe.matmul(bank, QS[0:ROW1 + 1, par, qt, c:c + P],
                                 KS[0:ROW1 + 1, par, kh, :], start=True, stop=True)
            else:
                for i in range(2):
                    o = bank[:, i * TOK:(i + 1) * TOK]
                    last = pe.matmul(o, QS[0:ROW1 + 1, par, qt, i * P:(i + 1) * P],
                                     KS[0:ROW1 + 1, par, kh, :], start=True, stop=name != 3)
                    if name == 3:
                        pe.matmul(o, IDR[:, :], MKS[:, par, HI, 0, i, :], start=False, stop=False)
                        last = pe.matmul(o, IDR[:, :], MKS[:, par, LO, 0, i, :], start=False, stop=True)
            last.then_inc(scores_ready, 1)

        def pe_rows(pe, b, s):
            v = unit(b, s, -1)
            wait(pe, act_done, v - 1)
            wait(pe, maxima_done, 4 * (NS * b + s) + 4)
            bank = AB[:, unit(0, s, -1) % 2, :]
            last = None
            for t in range(L.mtiles):
                for i in range(2):
                    o = bank[0:L.depth, t * WIN + i * P:t * WIN + (i + 1) * P]
                    last = pe.matmul(o, NM[:, s % 2, t, i, :], IDR[:, :], start=True, stop=True)
            last.then_inc(act_ready, 1)

        def pe_scores_t(pe, b, par, s, j):
            v = unit(b, s, j)
            qt, q0, kh = stacks_of(s, j)
            wait(pe, act_done, unit(b, s, -1) + 1 if s == 0 and j == 0 else v - 1)
            bank = AB[:, unit(0, s, j) % 2, :]
            last = None
            for kk in range(2):
                k = 2 * (j % 2) + kk if name == 0 else kk
                o = bank[:, kk * WIN:(kk + 1) * WIN]
                last = pe.matmul(o, KS[0:L.depth, par, kh, k * P:(k + 1) * P],
                                 QS[0:L.depth, par, qt, q0:q0 + WIN], start=True, stop=name != 3)
                if name == 3:
                    pe.matmul(o, IDR[:, :], MKS[:, par, HI, 1, k, :], start=False, stop=False)
                    last = pe.matmul(o, IDR[:, :], MKS[:, par, LO, 1, k, :], start=False, stop=True)
            last.then_inc(act_ready, 1)

        def pe_attend(pe, b, par, s, a):
            if a == 0:
                wait(pe, norm_done, NS * b + s)
            wait(pe, act_done, unit(b, s, 2 * a + 1 if name == 0 else a) + 1)
            kh = stacks_of(s, 2 * a if name == 0 else a)[2]
            last = None
            for i in range(2):
                o = OB[:, s % 2, (2 * a + i) * (L.dv + 1):(2 * a + i + 1) * (L.dv + 1)]
                for k in range(L.kt):
                    c = (k % 2) * WIN + i * P
                    last = pe.matmul(o, PR[:, s % 2, 2 * a + k // 2 if name == 0 else a, c:c + P],
                                     V[:, par, k, kh, :], start=k == 0, stop=k == L.kt - 1)
            if a == L.heads - 1:
                last.then_inc(av_done, 1)

        def pe_job(pe, job, k, par, jbase):
            wait(pe, bank_free[k % 2], count_before(jbase, k))
            bank = FB[:, k % 2, :]
            n = int(job[-1])
            last = None
            if job[:2] in ("XT", "CT", "AT"):
                src = {"XT": XF, "CT": CF, "AT": AO}[job[:2]]
                for f in range(2):
                    for t in range(2):
                        c = (2 * n + f) * P
                        last = pe.transpose(bank[:, f * TOK + t * P:f * TOK + (t + 1) * P],
                                            src[:, t, c:c + P], IDF[:, :])
            elif job[0] in "QK":
                w, x = (WQ, XS) if job[0] == "Q" else (WK, CS)
                tiles = 1 if name == 0 or (job[0] == "K" and name == 3) else 2
                width = DM if name == 0 else TOK
                for f in range(tiles):
                    c = (tiles * n + f) * P
                    last = exact_product(pe, bank[:, f * width:(f + 1) * width],
                                         lambda k_, h: w[:, h, k_, c:c + P],
                                         lambda k_, h: x[:, h, k_, :], kin)
            elif job[0] == "V":
                per = {0: TOK, 3: P}.get(name, DM)
                tiles = 1 if per == DM else 2
                for t in range(tiles):
                    k0 = (n * tiles + t) * P
                    last = exact_product(pe, bank[:, t * per:(t + 1) * per],
                                         lambda k_, h: CS[:, h, k_, k0:k0 + P],
                                         lambda k_, h: WV[:, h, k_, :], kin)
            elif job[0] == "O":
                last = exact_product(pe, bank, lambda k_, h: XS[:, h, k_, n * P:(n + 1) * P],
                                     lambda k_, h: WO[:, h, k_, :], kin)
            else:
                off = TOK if job[:3] == "STD" else 0
                for t in range(4):
                    last = pe.transpose(bank[:, t * P:(t + 1) * P],
                                        AO[:, t, off + n * P:off + (n + 1) * P], IDF[:, :])
            last.then_inc(job_ready, 1)

        def pe_head(pe, e, par, jbase, sbase, between=None):
            for k, job in enumerate(heads_jobs):
                if name == 0:
                    if job == "Q0":
                        wait(pe, x_lo, 2 * e + 1)
                    elif job == "V0":
                        wait(pe, x_lo, 2 * e + 2)
                elif job == "XT0":
                    if name == 2:
                        wait(pe, ln_done, 4 * e + 4)
                    else:
                        wait(pe, in_x, 16 * (e + 1))
                elif job == "CT0":
                    wait(pe, ln_done, 4 * e + 4)
                elif job == "Q0":
                    wait(pe, lo_done, sbase + split_index["XT1"] + 1)
                elif job == "K0":
                    if name == 1:
                        wait(pe, lo_done, sbase + split_index["CT1"] + 1)
                    else:
                        wait(pe, x_lo, e + 1)
                pe_job(pe, job, k, par, jbase)
                if k == 0 and between is not None:
                    between()

        def pe_first(pe, b, it, par):
            for n in range(2):
                wait(pe, nat_moved[n], 16 * per_head[n] * (b + 1))
            if name == 3:
                wait(pe, m_lo, b + 1)
            else:
                wait(pe, m_moved[par], 16 * (it + 1))
            for s in range(2):
                for j in range(4):
                    pe_scores(pe, b, par, s, j)

        def pe_section(pe, b, it, par, jbase, sbase, head, final):
            if name == 0:
                wait(pe, v_ready, V_JOBS * (b + 1))
            for s in range(NS):
                for j in range(4):
                    if s + 2 < NS:
                        pe_scores(pe, b, par, s + 2, j)
                    pe_scores_t(pe, b, par, s, j)
                    if j == 1 and s + 1 < NS:
                        pe_rows(pe, b, s + 1)
                    if name == 0:
                        if j == 0 and s > 0:
                            pe_attend(pe, b, par, s - 1, 1)
                        if j == 2:
                            pe_attend(pe, b, par, s, 0)
                    elif j == 0:
                        if s > 0:
                            pe_attend(pe, b, par, s - 1, L.heads - 1)
                    else:
                        pe_attend(pe, b, par, s, j - 1)
            kt = 0
            if head:
                pe_head(pe, b + 2, par, jbase, sbase,
                        lambda: pe_attend(pe, b, par, NS - 1, L.heads - 1))
                kt = NH
            else:
                pe_attend(pe, b, par, NS - 1, L.heads - 1)
            st = sbase + (SH if head else 0)
            if name:
                wait(pe, norm_done, NS * (b + 1) + 1)
                for k in range(2):
                    pe_job(pe, tail_jobs[k], kt + k, par, jbase)
            if not final:
                pe_first(pe, b + 1, it + par, 1 - par)
            if name:
                wait(pe, lo_done, st + 2)
                pe_job(pe, tail_jobs[2], kt + 2, par, jbase)
            else:
                wait(pe, root_done, 2 * (b + 1))
                for k in range(3):
                    pe_job(pe, tail_jobs[k], kt + k, par, jbase)
            if not final:
                pe_rows(pe, b + 1, 0)
            pe_job(pe, tail_jobs[3], kt + 3, par, jbase)

        def act_rows(act, b, par, s):
            qt, q0, _ = stacks_of(s, 0)
            v = unit(b, s, -1)
            act.wait_ge(act_ready, v + 1)
            bank = AB[ROW1:L.depth, unit(0, s, -1) % 2, :]
            out_ = QS[ROW1:L.depth, par, qt:qt + L.tiles, q0:q0 + WIN]
            if name == 3:
                src = bank.rearrange("p (t n) -> p t n", t=2)
            else:
                src = bank[:, 0:WIN].rearrange("p (t n) -> p t n", t=1)
                if L.tiles > 1:
                    src = src.to_broadcast([L.rows + 1, L.tiles, WIN])
            act.activation(out_, src, ACT.Copy).then_inc(act_done, 1)

        def act_exp(act, b, s, j):
            if j == 0:
                act.wait_ge(av_done, NS * b + s)
            act.wait_ge(act_ready, unit(b, s, j) + 1)
            act.activation(PR[:, s % 2, j, :], AB[:, unit(0, s, j) % 2, :], ACT.Exp,
                           scale=L.scale).then_inc(act_done, 1)

        def act_split(act, job, k, jbase, sbase):
            z = split_index[job] if job[:2] != "AT" or k >= NH else split_index[job] - SH
            slot = split_index[job] % 2
            n = int(job[-1])
            act.wait_ge(job_ready, J(jbase) + k + 1)
            wait(act, lo_done, sbase + z - (0 if z == 0 and SJ % 2 else 1))
            bank, dst = FB[:, k % 2, :], TMP[:, slot, :]
            if job[:2] in ("XT", "CT", "AT") and not (job[:2] == "XT" and name == 2) and job[:2] != "CT":
                act.activation(dst, bank, ACT.Copy).then_inc(bank_free[k % 2], 1)
            elif job[:2] in ("XT", "CT"):
                for f in range(2):
                    last = act.activation(dst[:, f * TOK:(f + 1) * TOK], bank[:, f * TOK:(f + 1) * TOK],
                                          ACT.Identity, bias=B1[:, 2 * n + f:2 * n + f + 1],
                                          scale=G1[:, 2 * n + f:2 * n + f + 1])
                last.then_inc(bank_free[k % 2], 1)
            elif name == 1:
                act.activation(dst, bank, ACT.Copy).then_inc(bank_free[k % 2], 1)
            else:
                bias = BQ if job[0] == "Q" else BK
                tiles = 1 if name == 0 or (job[0] == "K" and name == 3) else 2
                width = DM if name == 0 else TOK
                scale = 0.25 if job[0] == "Q" and name == 3 else 1.0
                for f in range(tiles):
                    m = tiles * n + f
                    last = act.activation(dst[:, f * width:(f + 1) * width],
                                          bank[:, f * width:(f + 1) * width],
                                          ACT.Identity, bias=bias[:, m:m + 1], scale=scale)
                last.then_inc(bank_free[k % 2], 1)

        def act_head(act, e, par, jbase, sbase, avs):
            for k, job in enumerate(heads_jobs):
                if job[0] != "V":
                    act_split(act, job, k, jbase, sbase)
                elif name == 1:
                    act.wait_ge(job_ready, J(jbase) + k + 1)
                    wait(act, av_done, avs)
                    act.activation(V[:, par, int(job[1]), :, 0:L.dv],
                                   FB[:, k % 2, :].rearrange("p (h d) -> p h d", d=L.dv),
                                   ACT.Copy).then_inc(bank_free[k % 2], 1)

        def act_section(act, b, it, par, jbase, sbase, head, final):
            for s in range(NS):
                for j in range(4):
                    act_exp(act, b, s, j)
                    if j == 1 and s + 1 < NS:
                        act_rows(act, b, par, s + 1)
                if name == 0 and s == 6:
                    act.wait_ge(masked_done, 2 * (b + 1))
                    for n in range(5):
                        wait(act, sums_done, 5 * b + n)
                        src = QM[:, :] if n == 4 else XR[:, n % 2, :]
                        act.activation(SQ[:, :], src, ACT.Square if n in (2, 3) else ACT.Copy,
                                       accum_out=ST8[:, n:n + 1]).then_inc(sums_done, 1)
            kt = 0
            if head:
                act_head(act, b + 2, par, jbase, sbase, NS * (b + 1) + 1)
                kt = NH
            if name:
                for k in range(2):
                    act_split(act, tail_jobs[k], kt + k, jbase, sbase)
            else:
                act.wait_ge(dev_done, 4 * (b + 1))
                act.activation(AO[:, :, TOK:2 * TOK], AO[:, :, TOK:2 * TOK], ACT.Relu).then_inc(root_done, 1)
                act.wait_ge(root_done, 2 * b + 1)
                act.activation(AO[:, :, TOK:2 * TOK], AO[:, :, TOK:2 * TOK], ACT.Sqrt).then_inc(root_done, 1)
            if not final:
                act_rows(act, b + 1, 1 - par, 0)

        def dve_max(dve, b, s, j):
            if j == 0:
                if s >= 2:
                    dve.wait_ge(act_ready, unit(b, s - 2, -1) + 1)
                elif not (isinstance(b, int) and b == 0):
                    dve.wait_ge(act_ready, unit(b - 1, NS - 2 + s, -1) + 1)
            dve.wait_ge(scores_ready, 4 * (NS * b + s) + j + 1)
            bank = SB[:, j % 2, :]
            if name == 0:
                src = bank
                dst = NM[:, s % 2, 0, j % 2, ROW1 + 1 + j // 2:ROW1 + 2 + j // 2]
            else:
                src = bank.rearrange("p (i n) -> p i n", i=2)
                t, r = (j // 2, j % 2) if name == 3 else (0, j)
                dst = NM[:, s % 2, t, :, ROW1 + 1 + r]
            dve.tensor_reduce(dst, src, AX.X, ALU.max, negate=True).then_inc(maxima_done, 1)

        def dve_norm(dve, b, s, jb):
            g = NS * b + s
            n = 2 * L.heads
            dve.wait_ge(av_done, g + 2)
            wait(dve, norm_done, g + 1)
            o = OB[:, s % 2, 0:n * (L.dv + 1)].rearrange("p (a c) -> p a c", c=L.dv + 1)
            dve.reciprocal(RC[:, :], o[:, :, L.dv]).then_inc(recip_done, 1)
            if s == 0:
                wait(dve, job_ready, jb)
            dve.wait_ge(recip_done, g + 1)
            last = None
            if name == 0:
                for a in range(2):
                    h = 2 * (s // 2) + a
                    for i in range(2):
                        src = o[:, 2 * a + i, 0:32].rearrange("p (k d) -> p k d", k=2)
                        dst = AO[:, 2 * (s % 2) + i, :].rearrange("p (k c) -> p k c", k=2)[:, :, 16 * h:16 * h + 16]
                        last = dve.tensor_scalar(dst, src, RC[:, 2 * a + i:2 * a + i + 1], None, ALU.mult)
            elif name == 3:
                for t in range(2):
                    h0 = 2 * (s // 2) * 4 + 2 * (s % 2) + t
                    src = o[:, 4 * t:4 * t + 4, 0:16].rearrange("p (a i) d -> p a i d", i=2)
                    rc = RC[:, 4 * t:4 * t + 4].rearrange("p (a i) -> p a i", i=2).unsqueeze(3).to_broadcast([P, 2, 2, 16])
                    dst = AO[:, :, :].rearrange("p i (h d) -> p h i d", d=16)[:, h0:h0 + 5:4]
                    last = dve.tensor_tensor(dst, src, rc, ALU.mult)
            else:
                src = o[:, :, 0:32].rearrange("p (a i) d -> p a i d", i=2)
                rc = RC[:, :].rearrange("p (a i) -> p a i", i=2).unsqueeze(3).to_broadcast([P, 4, 2, 32])
                dst = AO[:, :, :].rearrange("p i (h d) -> p h i d", d=32)[:, 4 * s:4 * s + 4]
                last = dve.tensor_tensor(dst, src, rc, ALU.mult)
            last.then_inc(norm_done, 1)

        def split_dst(job):
            n = int(job[-1])
            if job[:2] in ("XT", "AT"):
                return lambda h: XS[:, h, 2 * n:2 * n + 2, :]
            if job[:2] == "CT":
                return lambda h: CS[:, h, 2 * n:2 * n + 2, :]
            return lambda h: NAT[:, nat_slot[job], h, :]

        def shaped(job, ap):
            if job[0] == "K" and name == 3:
                return ap[:, 0:TOK]
            return ap.rearrange("p (f n) -> p f n", f=2) if job[1] == "T" else ap

        def cut(job, ap):
            return ap[:, 0:TOK] if job[0] == "K" and name == 3 else ap

        def dve_hi(dve, job, k, e, jbase, sbase):
            z = split_index[job] if job[:2] != "AT" or k >= NH else split_index[job] - SH
            dve.wait_ge(bank_free[k % 2], count_before(jbase, k) + 1)
            if job in nat_slot:
                wait(dve, nat_moved[nat_slot[job]], moved(job, e))
            dve.tensor_copy(cut(job, split_dst(job)(HI)), shaped(job, TMP[:, split_index[job] % 2, :])
                            ).then_inc(hi_done, 1)

        def dve_value(dve, job, k, e, par, jbase, avs):
            n = int(job[-1])
            dve.wait_ge(job_ready, J(jbase) + k + 1)
            wait(dve, av_done, avs)
            bank = FB[:, k % 2, :]
            if name == 2:
                last = dve.tensor_tensor(V[:, par, n, :, 0:32], bank.rearrange("p (h d) -> p h d", d=32),
                                         BV[:, :].rearrange("p (h d) -> p h d", d=32), ALU.add)
            else:
                w = TOK if name == 0 else P
                for t in range(2):
                    last = dve.tensor_tensor(V[:, par, 2 * n + t, :, 0:16],
                                             bank[:, t * w:(t + 1) * w].rearrange("p (h d) -> p h d", d=16),
                                             BV[:, :].rearrange("p (h d) -> p h d", d=16), ALU.add)
            last.then_inc(bank_free[k % 2], 1)

        def dve_head(dve, e, par, jbase, sbase, avs, between=None):
            for k, job in enumerate(heads_jobs):
                if job[0] != "V":
                    dve_hi(dve, job, k, e, jbase, sbase)
                elif name != 1:
                    dve_value(dve, job, k, e, par, jbase, avs)
                if k == 0 and between is not None:
                    between()

        def dve_prepare(dve, e, ite, pare, jfree):
            if name == 0:
                wait(dve, job_ready, jfree)
                dve.wait_ge(in_x, 16 * (e + 1))
                dve.tensor_copy(XS[:, HI, :, :], XF[:, :, :]).then_inc(x_hi, 1)
                dve.wait_ge(in_c, 16 * (e + 1))
                dve.tensor_copy(CS[:, HI, :, :], CF[:, :, :]).then_inc(x_hi, 1)
            elif name in (2, 3):
                wait(dve, job_ready, jfree)
                dve.wait_ge(in_c, 16 * (e + 1))
                dve.tensor_copy(CS[:, HI, :, :], CF[:, :, :].rearrange("p a (c n) -> p (a c) n", n=TOK)
                                ).then_inc(x_hi, 1)
            if name in (1, 2):
                R = CF if name == 1 else XF
                dve.wait_ge(in_c if name == 1 else in_x, 16 * (e + 1))
                for t in range(2):
                    dve.bn_stats(BN[:, t, :], R[:, t, :]).then_inc(ln_done, 1)
                wait_apart(dve, ln_done, 4 * e + 2, dve_passed)
                for t in range(2):
                    last = dve.bn_aggr(MV[:, t, :], BN[:, t, :])
                last.then_inc(ln_done, 1)
                dve.wait_ge(rstd_done, 2 * e + 2)
                for t in range(2):
                    last = dve.tensor_scalar(R[:, t, :], R[:, t, :], MV[:, t, 0:1], RS[:, t:t + 1],
                                             ALU.subtract, ALU.mult)
                last.then_inc(ln_done, 1)
            if name != 3:
                row = slice(ROW1, ROW1 + 1)
                dve.wait_ge(in_m, 16 * (e + 1))
                if not (isinstance(e, int) and e == 0):
                    n_before = ite + pare if not isinstance(ite, int) else (e - 1) // 2 + 1
                    dve.wait_ge(m_moved[1 - pare], 16 * n_before)
                if name == 2:
                    dve.tensor_scalar(MRR[row, :], MU8[row, :], 1.0, -NEG, ALU.subtract,
                                      ALU.mult).then_inc(m_row, 1)
                else:
                    dve.tensor_scalar(MRF[row, :], MU8[row, :], 1.0, 3.0e38, ALU.subtract,
                                      ALU.mult).then_inc(m_row, 1)
                    dve.wait_ge(m_row, 2 * e + 1)
                    dve.tensor_scalar(MRR[row, :], MRF[row, :], 10.0, None, ALU.mult).then_inc(m_row, 1)

        def dve_score_mask(dve, e, pare, taken):
            dve.wait_ge(in_m, 32 * (e + 1))
            wait(dve, m_lo, e)
            dve.tensor_scalar(MKC[:, :, :, :], MKF[:, :, :, :], NEG, None, ALU.max).then_inc(m_clamped, 1)
            wait(dve, act_ready, taken)
            dve.wait_ge(m_clamped, e + 1)
            dve.tensor_copy(MKS[:, pare, HI, :, :, :], MKC[:, :, :, :]).then_inc(m_hi, 1)

        def dve_instance_norm(dve, b):
            base = 7 * b
            dve.wait_ge(sums_done, 5 * (b + 1))
            dve.reciprocal(ST8[:, 4:5], ST8[:, 4:5]).then_inc(xn_done, 1)
            dve.wait_ge(xn_done, base + 1)
            dve.tensor_scalar(ST8[:, 0:4], ST8[:, 0:4], ST8[:, 4:5], None, ALU.mult).then_inc(xn_done, 1)
            dve.wait_ge(xn_done, base + 2)
            dve.tensor_tensor(ST8[:, 6:8], ST8[:, 0:2], ST8[:, 0:2], ALU.mult).then_inc(xn_done, 1)
            dve.wait_ge(xn_done, base + 3)
            dve.tensor_tensor(ST8[:, 6:8], ST8[:, 2:4], ST8[:, 6:8], ALU.subtract).then_inc(xn_done, 1)
            dve.wait_ge(xn_done, base + 4)
            dve.tensor_scalar(ST8[:, 6:8], ST8[:, 6:8], 0.0, 1e-5, ALU.max, ALU.add).then_inc(xn_done, 1)
            dve.wait_ge(xrstd_done, b + 1)
            for i in range(2):
                dve.tensor_scalar(XR[:, i, :], XR[:, i, :], ST8[:, i:i + 1], ST8[:, 8 + i:9 + i],
                                  ALU.subtract, ALU.mult).then_inc(xn_done, 1)

        def dve_tail(dve, b, kt, jbase, ks):
            for k in ks:
                job, n = tail_jobs[k], int(tail_jobs[k][-1])
                dve.wait_ge(job_ready, J(jbase) + kt + k + 1)
                bank = FB[:, (kt + k) % 2, :]
                y = XR[:, n, :]
                if name == 0:
                    if job[:3] == "STD":
                        dve.wait_ge(xn_done, 7 * (b + 1))
                    else:
                        dve.wait_ge(bank_free[(kt + k - 1) % 2], count_before(jbase, kt + k - 1) + 1)
                    last = dve.tensor_tensor(y, bank, y, ALU.mult if job[:3] == "STD" else ALU.add)
                elif name == 1:
                    dve.wait_ge(in_r, 16 * (b + 1))
                    last = dve.scalar_tensor_tensor(y, bank, GT[:, 0:1], y, ALU.mult, ALU.add)
                else:
                    dve.wait_ge(res_biased, b + 1)
                    last = dve.tensor_tensor(y, bank, y, ALU.add)
                last.then_inc(bank_free[(kt + k) % 2], 1)
            if name == 3 and 3 in ks:
                for n in range(2):
                    k = kt + 2 + n
                    dve.wait_ge(bank_free[k % 2], count_before(jbase, k) + 1)
                for t in range(2):
                    dve.bn_stats(BN[:, t, :], XR[:, t, :]).then_inc(ln_done, 1)
                wait_apart(dve, ln_done, 6 * b + 2, dve_passed)
                for t in range(2):
                    last = dve.bn_aggr(MV[:, t, :], BN[:, t, :])
                last.then_inc(ln_done, 1)
                dve.wait_ge(rstd_done, 2 * b + 2)
                for t in range(2):
                    last = dve.tensor_scalar(XR[:, t, :], XR[:, t, :], MV[:, t, 0:1], RS[:, t:t + 1],
                                             ALU.subtract, ALU.mult)
                last.then_inc(ln_done, 1)
                dve.wait_ge(ln_done, 6 * b + 4)
                dve.tensor_tensor(XR[:, :, :], XR[:, :, :], GA[:, :].unsqueeze(1).to_broadcast([P, 2, DM]),
                                  ALU.mult).then_inc(ln_done, 1)
                dve.wait_ge(ln_done, 6 * b + 5)
                dve.tensor_tensor(XR[:, :, :], XR[:, :, :], BE[:, :].unsqueeze(1).to_broadcast([P, 2, DM]),
                                  ALU.add).then_inc(ln_done, 1)

        def dve_section(dve, b, it, par, jbase, sbase, head, final):
            prep_at = 1 if NS == 4 else 3
            for s in range(NS):
                for j in range(4):
                    if s + 2 < NS:
                        dve_max(dve, b, s + 2, j)
                    if j == 1 and s > 0:
                        dve_norm(dve, b, s - 1, J(jbase))
                if s == prep_at and head:
                    dve_prepare(dve, b + 2, it + 1, par, J(jbase))
                if s == 1 and name == 0:
                    dve.wait_ge(in_r, 32 * (b + 1))
                    dve.tensor_copy(QM[:, :], QM8[:, :]).then_inc(qmask_done, 1)
                if name == 0 and s == 8:
                    dve_instance_norm(dve, b)
            kt = 0
            if head and name == 3:
                dve_score_mask(dve, b + 2, par, UB * (b + 1))
            if head:
                dve_head(dve, b + 2, par, jbase, sbase, NS * (b + 1) + 1,
                         lambda: dve_norm(dve, b, NS - 1, J(jbase)))
                kt = NH
            else:
                dve_norm(dve, b, NS - 1, J(jbase))
            if name:
                for k in range(2):
                    dve_hi(dve, tail_jobs[k], kt + k, b, jbase, sbase)
            if not final:
                for s in range(2):
                    for j in range(4):
                        dve_max(dve, b + 1, s, j)
            dve_tail(dve, b, kt, jbase, (2, 3) if name else (0, 1, 2, 3))

        def pool_lo(pool, job, sbase, head):
            z = split_index[job] - (SH if job[:2] == "AT" and not head else 0)
            pool.wait_ge(hi_done, sbase + z + 1)
            d = split_dst(job)
            pool.tensor_tensor(cut(job, d(LO)), shaped(job, TMP[:, split_index[job] % 2, :]),
                               cut(job, d(HI)).bitcast(F32), ALU.subtract).then_inc(lo_done, 1)

        def pool_head(pool, e, par, sbase, between=None):
            nv = 0
            for k, job in enumerate(heads_jobs):
                if job[0] != "V":
                    pool_lo(pool, job, sbase, True)
                elif name == 0:
                    n = int(job[1])
                    pool.wait_ge(bank_free[k % 2], between(k))
                    v = V[:, par, 2 * n:2 * n + 2, :, :].rearrange("p t h d -> p (t h) d")
                    pool.tensor_tensor(v[:, :, 16:32], v[:, :, 0:16], v[:, :, 0:16],
                                       ALU.mult).then_inc(v_ready, 1)

        def pool_prepare(pool, e):
            if name == 0:
                for n, (s_, r_) in enumerate(((XS, XF), (CS, CF))):
                    pool.wait_ge(x_hi, 2 * e + n + 1)
                    pool.tensor_tensor(s_[:, LO, :, :], r_[:, :, :], s_[:, HI, :, :].bitcast(F32),
                                       ALU.subtract).then_inc(x_lo, 1)
            elif name in (2, 3):
                pool.wait_ge(x_hi, e + 1)
                pool.tensor_tensor(CS[:, LO, :, :], CF[:, :, :].rearrange("p a (c n) -> p (a c) n", n=TOK),
                                   CS[:, HI, :, :].bitcast(F32), ALU.subtract).then_inc(x_lo, 1)
            if name in (1, 2):
                pool.wait_ge(ln_done, 4 * e + 3)
                pool.tensor_tensor(RS[:, :], MV[:, :, 1], CONST[:, 1:2].to_broadcast([P, 2]), ALU.add).then_inc(rstd_done, 1)
                pool.wait_ge(rstd_done, 2 * e + 1)
                pool.tensor_tensor(RS[:, :], RS[:, :], CONST[:, 0:1].to_broadcast([P, 2]),
                                   ALU.pow).then_inc(rstd_done, 1)

        def pool_mask_lo(pool, e, pare):
            pool.wait_ge(m_hi, e + 1)
            pool.tensor_tensor(MKS[:, pare, LO, :, :, :], MKC[:, :, :, :],
                               MKS[:, pare, HI, :, :, :].bitcast(F32), ALU.subtract).then_inc(m_lo, 1)

        def pool_variances(pool, b, f):
            pool.wait_ge(norm_done, NS * b + (f + 1) * NS // 2 + 1)
            mean = AO[:, :, f * P:(f + 1) * P]
            var = AO[:, :, TOK + f * P:TOK + (f + 1) * P]
            sq = SQ[:, :].rearrange("p (t n) -> p t n", t=4)
            base = 4 * b + 2 * f
            if f == 0:
                pool.wait_ge(sums_done, 5 * (b + 1))
            else:
                pool.wait_ge(dev_done, base)
            pool.tensor_tensor(sq, mean, mean, ALU.mult).then_inc(dev_done, 1)
            pool.wait_ge(dev_done, base + 1)
            pool.tensor_tensor(var, var, sq, ALU.subtract).then_inc(dev_done, 1)

        def pool_section(pool, b, it, par, jbase, sbase, head, final):
            if head:
                pool_prepare(pool, b + 2)
            if name == 0:
                pool.wait_ge(qmask_done, b + 1)
                for i in range(2):
                    pool.tensor_tensor(XR[:, i, :], XR[:, i, :], QM[:, :], ALU.mult).then_inc(masked_done, 1)
                pool.wait_ge(xn_done, 7 * b + 5)
                pool.tensor_tensor(ST8[:, 8:10], ST8[:, 6:8], CONST[:, 0:1].to_broadcast([P, 2]),
                                   ALU.pow).then_inc(xrstd_done, 1)
                pool_variances(pool, b, 0)
            if name in (2, 3):
                pool.wait_ge(in_r, 16 * (b + 1))
                pool.tensor_tensor(XR[:, :, :], XR[:, :, :], BO[:, :].unsqueeze(1).to_broadcast([P, 2, DM]),
                                   ALU.add).then_inc(res_biased, 1)
            if head and name == 3:
                pool_mask_lo(pool, b + 2, par)
            if head:
                pool_head(pool, b + 2, par, sbase, lambda k: count_before(jbase, k) + 1)
            if name:
                for k in range(2):
                    pool_lo(pool, tail_jobs[k], sbase, head)
            if name == 0:
                pool_variances(pool, b, 1)
                kt = NH if head else 0
                for n in range(2):
                    k = kt + 2 * n + 1
                    pool.wait_ge(bank_free[k % 2], count_before(jbase, k) + 1)
                    pool.tensor_tensor(XR[:, n, :], XR[:, n, :], QM[:, :], ALU.mult).then_inc(y_ready, 1)
            if name == 3:
                pool.wait_ge(ln_done, 6 * b + 3)
                pool.tensor_tensor(RS[:, :], MV[:, :, 1], CONST[:, 1:2].to_broadcast([P, 2]), ALU.add).then_inc(rstd_done, 1)
                pool.wait_ge(rstd_done, 2 * b + 1)
                pool.tensor_tensor(RS[:, :], RS[:, :], CONST[:, 0:1].to_broadcast([P, 2]),
                                   ALU.pow).then_inc(rstd_done, 1)

        tiles2 = lambda a: a.rearrange("(i p) n -> p i n", p=P)

        def sp_load(sp, e, par, jfree):
            if name == 0:
                wait_apart(sp, x_lo, 2 * e, sp_passed)
            else:
                wait_apart(sp, job_ready, jfree, sp_passed)
                if name in (2, 3):
                    wait_apart(sp, x_lo, e, sp_passed)
            sp.dma_start(XF[:, :, :], tiles2(x_in[e])).then_inc(in_x, 16)
            if name in (0, 1):
                sp.dma_start(CF[:, :, :], tiles2(ctx_in[e])).then_inc(in_c, 16)
            else:
                sp.dma_start(CF[:, :, :].rearrange("p a (c n) -> p (a c) n", n=TOK),
                             D["ctx_t"][e].rearrange("(c p) n -> p c n", p=P)).then_inc(in_c, 16)
            if name == 3:
                wait_apart(sp, m_clamped, e, sp_passed)
                sp.dma_start(MKF[:, 0, :, :], tiles2(D["mask"][e])).then_inc(in_m, 16)
                sp.dma_start(MKF[:, 1, :, :], tiles2(D["mask_t"][e])).then_inc(in_m, 16)
            else:
                wait_apart(sp, m_row, (1 if name == 2 else 2) * e, sp_passed)
                sp.dma_start(MU8[ROW1:ROW1 + 1, :], D["mask"][e]).then_inc(in_m, 16)

        def sp_move(sp, e, par, sbase):
            if name != 3:
                wait_apart(sp, m_row, (1 if name == 2 else 2) * (e + 1), sp_passed)
                src = words(MRR[ROW1:ROW1 + 1, :]).unsqueeze(1).to_broadcast([1, L.kv_heads, L.keys])
                sp.dma_start(words(KS[ROW1:ROW1 + 1, par, :, :]), src).then_inc(m_moved[par], 16)
            for job in nat_slot:
                n, slot = int(job[1]), nat_slot[job]
                wait_apart(sp, lo_done, sbase + split_index[job] + 1, sp_passed)
                parts = (HI, LO, HI) if job[0] == "Q" else (HI, HI, LO)
                dst_all = QS if job[0] == "Q" else KS
                for quad, part in enumerate(parts):
                    for r in range(4):
                        if job[0] == "K" and name in (0, 3):
                            for half in range(2):
                                lo_row = 16 * half + 32 * quad
                                head_ = (8 * n if name == 0 else 0) + 2 * r + half
                                sp.dma_start(words(KS[lo_row:lo_row + 16, par, head_, :]), words(
                                    NAT[32 * r + 16 * half:32 * r + 16 * half + 16, slot, part, 0:L.keys])
                                             ).then_inc(nat_moved[slot], 16)
                            continue
                        src = NAT[32 * r:32 * r + 32, slot, part, :]
                        rows = slice(32 * quad, 32 * quad + 32)
                        if name == 0:
                            dst = dst_all[rows, par, 4 * n + r, :]
                        elif name == 3:
                            dst = dst_all[rows, par, 4 * r + 2 * n:4 * r + 2 * n + 2, :]
                            src = src.rearrange("p (f n) -> p f n", f=2)
                        else:
                            dst = dst_all[rows, par, 8 * n + r:8 * n + r + 5:4, :]
                            src = src.rearrange("p (f n) -> p f n", f=2)
                        sp.dma_start(words(dst), words(src)).then_inc(nat_moved[slot], 16)

        def sp_section(sp, b, it, par, jbase, sbase, head, final):
            if head:
                sp_load(sp, b + 2, par, J(jbase))
            wait_apart(sp, y_stored, 16 * b, sp_passed)
            sp.dma_start(XR[:, :, :], tiles2(x_in[b])).then_inc(in_r, 16)
            if name == 0:
                wait_apart(sp, y_ready, 2 * b, sp_passed)
                sp.dma_start(QM8[:, :], D["mask_rows"][b].partition_broadcast(P)).then_inc(in_r, 16)
            if head:
                wait_apart(sp, act_ready, UB * (b + 1), sp_passed)
                sp_move(sp, b + 2, par, sbase)
            if name == 0:
                wait_apart(sp, y_ready, 2 * (b + 1), sp_passed)
            elif name == 3:
                wait_apart(sp, ln_done, 6 * (b + 1), sp_passed)
            else:
                kt = NH if head else 0
                for k in (kt + 2, kt + 3):
                    wait_apart(sp, bank_free[k % 2], count_before(jbase, k) + 1, sp_passed)
            sp.dma_start(tiles2(out[b]), XR[:, :, :]).then_inc(y_stored, 16)

        def sections(eng, section):
            with eng.Fori(0, NB // 2 - 1) as it:
                for par in range(2):
                    b = it * 2 + par
                    jbase = (b * NJ + 2 * NH, b * (NJ // 2) + NH)
                    section(eng, b, it, par, jbase, b * SJ + 2 * SH, True, False)
            b, it = NB - 2, NB // 2 - 1
            section(eng, b, it, 0, 2 * NH + NJ * b, 2 * SH + SJ * b, False, False)
            section(eng, b + 1, it, 1, 2 * NH + NJ * b + NT, 2 * SH + SJ * b + SJ - SH, False, True)

        if name == 3:
            with nc.Block() as block:
                @block.vector
                def _(dve):
                    dve.tensor_scalar(BQ[:, :], BQ[:, :], 0.25, None, ALU.mult).then_inc(c_set, 1)

        with nc.Block() as block:
            @block.sync
            def _(sp):
                for e in range(2):
                    sp_load(sp, e, e, NH * e)
                    sp_move(sp, e, e, SH * e)
                sections(sp, sp_section)
                sp.wait_ge(y_stored, 16 * NB)

            @block.tensor
            def _(pe):
                pe.sem_inc(av_done, 1)
                for e in range(2):
                    pe_head(pe, e, e, NH * e, SH * e)
                pe_first(pe, 0, 0, 0)
                pe_rows(pe, 0, 0)
                sections(pe, pe_section)

            @block.scalar
            def _(act):
                for e in range(2):
                    act_head(act, e, e, NH * e, SH * e, 0)
                act_rows(act, 0, 0, 0)
                sections(act, act_section)

            @block.vector
            def _(dve):
                dve.sem_inc(norm_done, 1)
                for e in range(2):
                    dve_prepare(dve, e, 0, e, NH * e)
                    if name == 3:
                        dve_score_mask(dve, e, e, 0)
                    dve_head(dve, e, e, NH * e, SH * e, 0)
                for s in range(2):
                    for j in range(4):
                        dve_max(dve, 0, s, j)
                sections(dve, dve_section)

            @block.gpsimd
            def _(pool):
                for e in range(2):
                    pool_prepare(pool, e)
                    if name == 3:
                        pool_mask_lo(pool, e, e)
                    pool_head(pool, e, e, SH * e, lambda k, e=e: count_before(NH * e, k) + 1)
                sections(pool, pool_section)

        give_back(nc, used)


def feed_forward(nc, NB, A, x_in, out):
    FT = DM // P
    HT = INNER // P
    FJ = HT // 2
    with ExitStack() as ctx:
        def sb(n, shape, dt):
            return ctx.enter_context(nc.sbuf_tensor(f"ff_{n}", shape, dt))

        used = []

        def sem(n):
            used.append(ctx.enter_context(nc.semaphore(f"ff_{n}")))
            return used[-1]

        WF = sb("fc", [P, 2, FT, INNER], F32R)
        WP = sb("proj", [P, 2, HT, DM], F32R)
        XF = sb("x_raw", [P, 2, DM], F32)
        XR = sb("x_residual", [P, 2, 2, DM], F32)
        XT = sb("x_transposed", [P, 2, DM], F32)
        XS = sb("x_split", [P, 2, FT, TOK], F32R)
        HF = sb("hidden_raw", [P, 4, BANK], F32)
        HS = sb("hidden_split", [P, 2, HT, TOK], F32R)
        IDF = sb("ident", [P, P], F32)
        CONST = sb("constants", [P, 2], F32)
        G2 = sb("norm_w", [P, FT], F32)
        B2 = sb("norm_b", [P, FT], F32)
        BF = sb("fc_bias", [P, HT], F32)
        BP = sb("proj_bias", [P, DM], F32)
        BN = sb("bn", [P, 2, 6], F32)
        MV = sb("mean_var", [P, 2, 2], F32)
        RS = sb("rstd", [P, 2], F32)
        HB = ctx.enter_context(nc.psum_tensor("ff_hidden", [P, 4, BANK], F32))
        TB = ctx.enter_context(nc.psum_tensor("ff_transposed", [P, 2, BANK], F32))
        YB = ctx.enter_context(nc.psum_tensor("ff_out", [P, 2, BANK], F32))

        c_load, c_set = sem("c_load"), sem("c_set")
        consts = [(G2[:, :], A["w4_ln_w"]), (B2[:, :], A["w4_ln_b"]), (BF[:, :], A["w4_fc_b"]),
                  (BP[:, :], A["w4_proj_b"].partition_broadcast(P))]
        with nc.Block() as block:
            @block.gpsimd
            def _(pool):
                pool.memset(IDF[:, :], 0.0).then_inc(c_set, 1)
                pool.memset(CONST[:, 0:1], -0.5)
                pool.memset(CONST[:, 1:2], 1e-5)
                pool.wait_ge(c_set, 1)
                pool.affine_select(out=IDF[:, :], in_=IDF[:, :], compare_op=ALU.not_equal, fill=1.0,
                                   base=0, pattern=[[-1, P]], channel_multiplier=1).then_inc(c_set, 1)

            @block.scalar
            def _(act):
                for dst, src in consts:
                    act.dma_start(dst, src).then_inc(c_load, 16)
                act.wait_ge(c_load, 16 * len(consts))

        fc = A["w4_fc"].rearrange("(k p) n -> p k n", p=P)
        parts = [(fc[:, :, q * DM:(q + 1) * DM], WF[:, :, :, q * DM:(q + 1) * DM]) for q in range(INNER // DM)]
        parts.append((A["w4_proj"].rearrange("(k p) n -> p k n", p=P), WP))
        split_weights(nc, sem, parts, HF)

        in_x = sem("in_x")
        in_r = [sem("in_r0"), sem("in_r1")]
        y_stored = [sem("y_stored0"), sem("y_stored1")]
        sp_passed, dve_passed = sem("sp_passed"), sem("dve_passed")
        ln_done = sem("ln_done")
        rstd_done = sem("rstd_done")
        xt_ready = sem("xt_ready")
        xt_taken = sem("xt_taken")
        x_hi, x_lo = sem("x_hi"), sem("x_lo")
        fc_ready = sem("fc_ready")
        gelu_done = sem("gelu_done")
        g_hi, g_lo = sem("g_hi"), sem("g_lo")
        res_biased = sem("res_biased")
        y_ready = sem("y_ready")
        y_done = sem("y_done")
        rows = lambda a: a.rearrange("(i p) n -> p i n", p=P)

        def pair(ap):
            return ap.rearrange("p (f n) -> p f n", f=2)

        def pe_transpose(pe, e):
            pe.wait_ge(ln_done, 4 * (e + 1))
            for n in range(2):
                wait(pe, xt_taken, 2 * e + n - 1)
                for f in range(2):
                    for t in range(2):
                        c = (2 * n + f) * P
                        last = pe.transpose(TB[:, n, f * TOK + t * P:f * TOK + (t + 1) * P],
                                            XF[:, t, c:c + P], IDF[:, :])
                last.then_inc(xt_ready, 1)

        def pe_section(pe, b, it, par, more):
            pe.wait_ge(x_lo, 2 * (b + 1))
            for m in range(FJ):
                wait(pe, gelu_done, FJ * b + m - 3)
                for f in range(2):
                    c = (2 * m + f) * P
                    last = exact_product(pe, HB[:, m % 4, f * TOK:(f + 1) * TOK],
                                         lambda k, h: WF[:, h, k, c:c + P],
                                         lambda k, h: XS[:, h, k, :], FT)
                last.then_inc(fc_ready, 1)
            if more:
                pe_transpose(pe, b + 1)
            for n in range(2):
                wait(pe, y_done, 2 * b + n - 1)
                for k in range(HT):
                    if n == 0 and k % 2 == 0:
                        pe.wait_ge(g_lo, FJ * b + k // 2 + 1)
                    last = exact_product(pe, YB[:, n, :], lambda _, h: HS[:, h, k, n * P:(n + 1) * P],
                                         lambda _, h: WP[:, h, k, :], 1, start=k == 0, stop=k == HT - 1)
                last.then_inc(y_ready, 1)

        def act_transposed(act, e):
            for n in range(2):
                act.wait_ge(xt_ready, 2 * e + n + 1)
                wait(act, x_lo, 2 * e + n - 1)
                for f in range(2):
                    m = 2 * n + f
                    last = act.activation(XT[:, n, f * TOK:(f + 1) * TOK], TB[:, n, f * TOK:(f + 1) * TOK],
                                          ACT.Identity, bias=B2[:, m:m + 1], scale=G2[:, m:m + 1])
                last.then_inc(xt_taken, 1)

        def act_section(act, b, it, par, more):
            for m in range(FJ):
                act.wait_ge(fc_ready, FJ * b + m + 1)
                wait(act, g_lo, FJ * b + m - 3)
                for f in range(2):
                    h = 2 * m + f
                    last = act.activation(HF[:, m % 4, f * TOK:(f + 1) * TOK],
                                          HB[:, m % 4, f * TOK:(f + 1) * TOK],
                                          ACT.Gelu_apprx_tanh, bias=BF[:, h:h + 1])
                last.then_inc(gelu_done, 1)
            if more:
                act_transposed(act, b + 1)

        def dve_norm(dve, e):
            dve.wait_ge(in_x, 16 * (e + 1))
            for t in range(2):
                dve.bn_stats(BN[:, t, :], XF[:, t, :]).then_inc(ln_done, 1)
            wait_apart(dve, ln_done, 4 * e + 2, dve_passed)
            for t in range(2):
                last = dve.bn_aggr(MV[:, t, :], BN[:, t, :])
            last.then_inc(ln_done, 1)
            dve.wait_ge(rstd_done, 2 * e + 2)
            for t in range(2):
                last = dve.tensor_scalar(XF[:, t, :], XF[:, t, :], MV[:, t, 0:1], RS[:, t:t + 1],
                                         ALU.subtract, ALU.mult)
            last.then_inc(ln_done, 1)

        def dve_transposed(dve, e):
            for n in range(2):
                dve.wait_ge(xt_taken, 2 * e + n + 1)
                dve.tensor_copy(XS[:, HI, 2 * n:2 * n + 2, :], pair(XT[:, n, :])).then_inc(x_hi, 1)

        def dve_section(dve, b, it, par, more):
            for m in range(FJ):
                dve.wait_ge(gelu_done, FJ * b + m + 1)
                if m == 0:
                    wait(dve, y_ready, 2 * b)
                dve.tensor_copy(HS[:, HI, 2 * m:2 * m + 2, :], pair(HF[:, m % 4, :])).then_inc(g_hi, 1)
                if m == 3 and more:
                    dve_norm(dve, b + 1)
            if more:
                dve_transposed(dve, b + 1)
            dve.wait_ge(res_biased, b + 1)
            for n in range(2):
                dve.wait_ge(y_ready, 2 * b + n + 1)
                dve.tensor_tensor(XR[:, par, n, :], YB[:, n, :], XR[:, par, n, :], ALU.add).then_inc(y_done, 1)

        def pool_norm(pool, e):
            pool.wait_ge(ln_done, 4 * e + 3)
            pool.tensor_tensor(RS[:, :], MV[:, :, 1], CONST[:, 1:2].to_broadcast([P, 2]), ALU.add).then_inc(rstd_done, 1)
            pool.wait_ge(rstd_done, 2 * e + 1)
            pool.tensor_tensor(RS[:, :], RS[:, :], CONST[:, 0:1].to_broadcast([P, 2]), ALU.pow).then_inc(rstd_done, 1)

        def pool_transposed(pool, e):
            for n in range(2):
                pool.wait_ge(x_hi, 2 * e + n + 1)
                pool.tensor_tensor(XS[:, LO, 2 * n:2 * n + 2, :], pair(XT[:, n, :]),
                                   XS[:, HI, 2 * n:2 * n + 2, :].bitcast(F32), ALU.subtract).then_inc(x_lo, 1)

        def pool_section(pool, b, it, par, more):
            for m in range(FJ):
                pool.wait_ge(g_hi, FJ * b + m + 1)
                pool.tensor_tensor(HS[:, LO, 2 * m:2 * m + 2, :], pair(HF[:, m % 4, :]),
                                   HS[:, HI, 2 * m:2 * m + 2, :].bitcast(F32), ALU.subtract).then_inc(g_lo, 1)
                if m == 3 and more:
                    pool_norm(pool, b + 1)
            if more:
                pool_transposed(pool, b + 1)
            pool.wait_ge(in_r[par], 16 * (it + 1))
            pool.tensor_tensor(XR[:, par, :, :], XR[:, par, :, :],
                               BP[:, :].unsqueeze(1).to_broadcast([P, 2, DM]), ALU.add).then_inc(res_biased, 1)

        def sp_section(sp, b, it, par, more):
            if more:
                wait_apart(sp, xt_ready, 2 * (b + 1), sp_passed)
                sp.dma_start(XF[:, :, :], rows(x_in[b + 1])).then_inc(in_x, 16)
            wait_apart(sp, y_stored[par], 16 * it, sp_passed)
            sp.dma_start(XR[:, par, :, :], rows(x_in[b])).then_inc(in_r[par], 16)
            wait_apart(sp, y_done, 2 * (b + 1), sp_passed)
            sp.dma_start(rows(out[b]), XR[:, par, :, :]).then_inc(y_stored[par], 16)

        def sections(eng, section):
            for par in range(2):
                section(eng, par, 0, par, True)
            with eng.Fori(1, NB // 2 - 1) as it:
                for par in range(2):
                    section(eng, it * 2 + par, it, par, True)
            section(eng, NB - 2, NB // 2 - 1, 0, True)
            section(eng, NB - 1, NB // 2 - 1, 1, False)

        with nc.Block() as block:
            @block.sync
            def _(sp):
                sp.dma_start(XF[:, :, :], rows(x_in[0])).then_inc(in_x, 16)
                sections(sp, sp_section)
                for par in range(2):
                    sp.wait_ge(y_stored[par], 16 * (NB // 2))

            @block.tensor
            def _(pe):
                pe_transpose(pe, 0)
                sections(pe, pe_section)

            @block.scalar
            def _(act):
                act_transposed(act, 0)
                sections(act, act_section)

            @block.vector
            def _(dve):
                dve_norm(dve, 0)
                dve_transposed(dve, 0)
                sections(dve, dve_section)

            @block.gpsimd
            def _(pool):
                pool_norm(pool, 0)
                pool_transposed(pool, 0)
                sections(pool, pool_section)

        give_back(nc, used)


def views(layer, A):
    w = f"w{layer}_"
    D = {n: A[w + n] for n in ("wq", "wk", "wv")}
    if layer:
        D["wo"] = A[w + "wo"]
    if layer != 1:
        for n in ("bq", "bk", "bv"):
            D[n] = A[w + n]
    if layer == 0:
        D["mask"], D["mask_rows"] = A["mask_row"], A["mask_row"].rearrange("b a n -> b (a n)")
    elif layer in (1, 2):
        D["mask"] = A["key_mask"]
        D["ln_w"], D["ln_b"] = A[w + "ln_w"], A[w + "ln_b"]
    if layer == 1:
        D["gate"] = A[w + "gate"]
    if layer in (2, 3):
        D["bo"], D["ctx_t"] = A[w + "bo"], A["ctx_t"]
    if layer == 3:
        D["gamma"], D["beta"] = A[w + "gamma"], A[w + "beta"]
        D["mask"], D["mask_t"] = A["mask"], A["mask_t"]
    return D


def layouts(inputs):
    a = {k: np.asarray(v) for k, v in inputs.items()}
    c = np.ascontiguousarray
    cols = lambda v: c(v.reshape(-1, P).T)
    nb = a["x"].shape[0]
    by_member = lambda w: w.reshape(w.shape[:-1] + (8, 4, 16)).swapaxes(-3, -2).reshape(w.shape)
    out = {
        "x": c(a["x"]), "ctx": c(a["ctx_2048"]), "ctx_t": c(a["ctx_2048"].transpose(0, 2, 1)),
        "mask_row": c(a["mask_Bx1x2048_bf1"].view(np.uint8)),
        "key_mask": c(a["mask_BxS2_bf1"].view(np.uint8).reshape(nb, 1, -1)),
        "mask": c(a["mask_Bx1xSxS2_ff0"][:, 0]), "mask_t": c(a["mask_Bx1xSxS2_ff0"][:, 0].transpose(0, 2, 1)),
        "w0_wq": c(a["L0_xattn_Wq"].T), "w0_wk": c(a["L0_xattn_Wk"].T), "w0_wv": c(a["L0_xattn_Wv"].T),
        "w0_bq": cols(a["L0_xattn_bq"]), "w0_bk": cols(a["L0_xattn_bk"]), "w0_bv": c(a["L0_xattn_bv"]),
        "w1_wq": c(a["L1_xattn_Wq"].T), "w1_wk": c(a["L1_xattn_Wk"].T), "w1_wv": c(a["L1_xattn_Wv"].T),
        "w1_wo": c(a["L1_xattn_Wo"].T), "w1_ln_w": cols(a["L1_xattn_ln_gamma"]),
        "w1_ln_b": cols(a["L1_xattn_ln_beta"]), "w1_gate": c(a["L1_xattn_gate"]),
        "w2_wq": c(a["L2_xattn_q_w"]), "w2_wk": c(a["L2_xattn_k_w"]), "w2_wv": c(a["L2_xattn_v_w"]),
        "w2_wo": c(a["L2_xattn_cproj_w"]), "w2_bq": cols(a["L2_xattn_q_b"]), "w2_bk": cols(a["L2_xattn_k_b"]),
        "w2_bv": c(a["L2_xattn_v_b"]), "w2_bo": c(a["L2_xattn_cproj_b"]),
        "w2_ln_w": cols(a["L2_xattn_ln1_w"]), "w2_ln_b": cols(a["L2_xattn_ln1_b"]),
        "w4_ln_w": cols(a["L2_xattn_ln2_w"]), "w4_ln_b": cols(a["L2_xattn_ln2_b"]),
        "w4_fc": c(a["L2_xattn_fc_w"]), "w4_fc_b": cols(a["L2_xattn_fc_b"]),
        "w4_proj": c(a["L2_xattn_proj_w"]), "w4_proj_b": c(a["L2_xattn_proj_b"]),
        "w3_wq": c(by_member(a["L3_xattn_Wq"])), "w3_wk": c(a["L3_xattn_Wk"]), "w3_wv": c(a["L3_xattn_Wv"]),
        "w3_wo": c(a["L3_xattn_Wo"]), "w3_bq": cols(by_member(a["L3_xattn_bq"])),
        "w3_bk": cols(a["L3_xattn_bk"]), "w3_bv": c(a["L3_xattn_bv"]), "w3_bo": c(a["L3_xattn_bo"]),
        "w3_gamma": c(a["L3_xattn_gamma"]), "w3_beta": c(a["L3_xattn_beta"]),
    }
    return out


def build(nc, NB, A, out):
    shape = (NB, TOK, DM)
    x1 = nc.dram_tensor("x_after_layer0", shape, F32, kind="Internal").ap()
    x2 = nc.dram_tensor("x_after_layer1", shape, F32, kind="Internal").ap()
    x3 = nc.dram_tensor("x_after_attention2", shape, F32, kind="Internal").ap()
    x4 = nc.dram_tensor("x_after_layer2", shape, F32, kind="Internal").ap()
    attention_layer(nc, L0, NB, views(0, A), A["x"], A["ctx"], x1)
    attention_layer(nc, L1, NB, views(1, A), x1, A["ctx"], x2)
    attention_layer(nc, L2, NB, views(2, A), x2, A["ctx"], x3)
    feed_forward(nc, NB, A, x3, x4)
    attention_layer(nc, L3, NB, views(3, A), x4, A["ctx"], out)


def kernel(**inputs):
    from concourse import bacc, mybir as _mybir
    from concourse.bass_utils import run_bass_kernel_spmd
    arrays = layouts(inputs)
    nb = arrays["x"].shape[0]
    nc = bacc.Bacc("TRN2", target_bir_lowering=False, num_devices=1)
    A = {n: nc.dram_tensor(n, a.shape, _mybir.dt.from_np(a.dtype), kind="ExternalInput").ap()
         for n, a in arrays.items()}
    out = nc.dram_tensor("out", (nb, TOK, DM), F32, kind="ExternalOutput").ap()
    build(nc, nb, A, out)
    result = run_bass_kernel_spmd(nc, [arrays], core_ids=[0])
    return result.results[0]["out"]
```

```python
import numpy as np
from contextlib import ExitStack
import concourse.bass as bass
import concourse.mybir as mybir

F32 = mybir.dt.float32
F32R = mybir.dt.float32r
U8 = mybir.dt.uint8
ALU = mybir.AluOpType
ACT = mybir.ActivationFunctionType
AX = mybir.AxisListType

P = 128
TOK = 256
DM = 512
WIN = 256
BANK = 512
STACK = 96
ROW1 = 96
NEG = -1.0e30
INNER = 2048
HI, LO = 0, 1


class Layer:

    def __init__(self, name, keys, steps, row_steps, out_steps, tiles, rows, row_tiles, kv_heads,
                 q_tiles, q_width, scale):
        self.name = name
        self.keys = keys
        self.kt = keys // P
        self.steps = steps
        self.row_steps = row_steps
        self.out_steps = out_steps
        self.tiles = tiles
        self.rows = rows
        self.row_tiles = row_tiles
        self.depth = ROW1 + 1 + rows
        self.kv_heads = kv_heads
        self.q_tiles = q_tiles
        self.q_width = q_width
        self.scale = scale


L0 = Layer(0, DM, 16, 2, 2, 2, 4, 1, 16, 8, DM, 0.25)
L1 = Layer(1, TOK, 4, 1, 1, 4, 4, 1, 16, 16, TOK, 32 ** -0.5)
L2 = Layer(2, TOK, 4, 1, 1, 4, 4, 1, 16, 16, TOK, 32 ** -0.5)
L3 = Layer(3, TOK, 8, 1, 2, 1, 2, 2, 8, 16, TOK, 1.0)


def words(ap):
    return ap.bitcast(F32)


def wait(eng, sem, value):
    if isinstance(value, int) and value <= 0:
        return
    eng.wait_ge(sem, value)


def wait_apart(eng, sem, value, passed):
    wait(eng, sem, value)
    if not isinstance(value, int):
        eng.sem_inc(passed, 1)


def give_back(nc, used):
    with nc.Block() as block:
        @block.sync
        def _(sp):
            for s in used[0::3]:
                sp.sem_clear(s)

        @block.scalar
        def _(act):
            for s in used[1::3]:
                act.sem_clear(s)

        @block.vector
        def _(dve):
            for s in used[2::3]:
                dve.sem_clear(s)


def weight_steps(sem, weights, stage):
    slots = stage.shape[1]
    chunks = [(src[:, c, :], dst[:, HI, c, :], dst[:, LO, c, :], src.shape[2])
              for src, dst in weights for c in range(src.shape[1])]
    raw = [sem(f"wraw{i}") for i in range(slots)]
    hi_done = sem("whi")
    lo_done = sem("wlo")

    def load(sp):
        for n, (src, _, _, w) in enumerate(chunks):
            wait(sp, lo_done, n - slots + 1)
            sp.dma_start(stage[:, n % slots, 0:w], src).then_inc(raw[n % slots], 16)
        sp.wait_ge(lo_done, len(chunks))

    def high(act):
        for n, (_, hi, _, w) in enumerate(chunks):
            act.wait_ge(raw[n % slots], 16 * (n // slots + 1))
            act.activation(hi, stage[:, n % slots, 0:w], ACT.Copy).then_inc(hi_done, 1)

    def low(dve):
        for n, (_, hi, lo, w) in enumerate(chunks):
            dve.wait_ge(hi_done, n + 1)
            dve.tensor_tensor(lo, stage[:, n % slots, 0:w], hi.bitcast(F32),
                              ALU.subtract).then_inc(lo_done, 1)

    return load, high, low


def exact_product(pe, out, lhs, rhs, depth, start=True, stop=True):
    last = None
    for k in range(depth):
        for n, (a, b) in enumerate(((HI, HI), (HI, LO), (LO, HI))):
            last = pe.matmul(out, lhs(k, a), rhs(k, b), start=start and k == 0 and n == 0,
                             stop=stop and k == depth - 1 and n == 2)
    return last


def attention_layer(nc, L, NB, D, x_in, ctx_in, out):
    name = L.name
    NS = L.steps
    RS_, OS = L.row_steps, L.out_steps
    AHEAD = RS_ + 1
    NG = NS // OS
    UB = 4 * NS + NS // RS_
    heads_jobs = {0: ["Q0", "V0", "Q1", "V1", "K0", "K1"],
                  1: ["CT0", "CT1", "K0", "K1", "XT0", "XT1", "V0", "V1", "Q0", "Q1"],
                  2: ["K0", "K1", "XT0", "XT1", "V0", "V1", "Q0", "Q1"],
                  3: ["K0", "XT0", "XT1", "V0", "Q0", "Q1"]}[name]
    out_jobs = ["O0", "O1"] if name else []
    OUT_AT = {1: 4, 3: 1}.get(name, 2)
    section_jobs = heads_jobs[:OUT_AT] + out_jobs + heads_jobs[OUT_AT:]
    NH, NT = len(heads_jobs), len(out_jobs)
    MR = 2 if name == 1 else 1
    NJ = NH + NT
    split_head = [j for j in heads_jobs if j[0] != "V"]
    SH = len(split_head)
    LEAD = 4
    SLOTS = 3 if name else 4
    split_index = {j: n for n, j in enumerate(split_head)}

    with ExitStack() as ctx:
        def sb(n, shape, dt):
            return ctx.enter_context(nc.sbuf_tensor(f"l{name}_{n}", shape, dt))

        used = []

        def sem(n):
            used.append(ctx.enter_context(nc.semaphore(f"l{name}_{n}")))
            return used[-1]

        QS = sb("query_stack", [P, 2, L.q_tiles, L.q_width], F32R)
        KS = sb("key_stack", [P, 2, L.kv_heads, L.keys], F32R)
        VPAD = 16 if name == 3 else 0
        V = sb("values", [P, 2, L.kt, L.kv_heads * 32 + VPAD], F32)
        ONES = sb("ones", [P, 48], F32)
        PR = sb("probs", [P, 2, 4, BANK], F32)
        if name == 0:
            AO = sb("moments", [P, 2, 2, DM], F32)
            AF = sb("attended", [P, 2, DM], F32)
        else:
            AF = sb("attended", [P, 2, WIN], F32)
        NAT = sb("natural", [P, SLOTS, 2, BANK], F32R)
        TMP = sb("evacuated", [P, 2, BANK], F32)
        XF = sb("x_raw", [P, 2, DM], F32)
        CF = sb("ctx_raw", [P, 2, DM], F32) if name else XF
        XR = sb("x_residual", [P, 2, DM], F32)
        NM = sb("minus_max", [P, 2, L.row_tiles, 2, L.depth], F32R)
        RC = sb("reciprocals", [P, WIN], F32)
        IDF = sb("ident", [P, P], F32) if name else TMP[:, 0, 0:P]
        IDR = sb("ident_r", [P, P], F32R)
        CONST = sb("constants", [P, 2], F32)
        OHF = sb("onehot_f", [P, L.rows], F32)
        OHR = NAT[:, :, :, :].rearrange("p s h n -> p (s h n)")[:, 0:L.rows * L.keys].rearrange(
            "p (r n) -> p r n", r=L.rows)
        if name == 0:
            XS = sb("x_split", [P, 2, 2, DM], F32R)
            CS = sb("ctx_split", [P, 2, 2, DM], F32R)
        else:
            XS = sb("x_split", [P, 2, 4, TOK], F32R)
            CS = sb("ctx_split", [P, 2, 4, TOK], F32R)
        kin = 2 if name == 0 else 4
        wq_n = TOK if name == 0 else DM
        wk_n = {0: TOK, 3: P}.get(name, DM)
        WQ = sb("wq", [P, 2, kin, wq_n], F32R)
        WK = sb("wk", [P, 2, kin, wk_n], F32R)
        WV = sb("wv", [P, 2, kin, wk_n], F32R)
        weights = [(D["wq"].rearrange("(k p) n -> p k n", p=P), WQ),
                   (D["wk"].rearrange("(k p) n -> p k n", p=P), WK),
                   (D["wv"].rearrange("(k p) n -> p k n", p=P), WV)]
        if name:
            WO = sb("wo", [P, 2, 4, DM], F32R)
            weights.append((D["wo"].rearrange("(k p) n -> p k n", p=P), WO))
        if name != 1:
            BQ = sb("bq", [P, wq_n // P], F32)
            BK = sb("bk", [P, max(wk_n // P, 1)], F32)
            BV = sb("bv", [P, wk_n], F32)
        if name != 3:
            MU8 = sb("mask_bytes", [P, L.keys], U8)
            MRF = sb("mask_row_f", [P, L.keys], F32) if name == 1 else None
            MRR = sb("mask_row", [P, L.keys], F32R)
        if name == 0:
            QM8 = sb("query_mask_bytes", [P, DM], U8)
            QM = sb("query_mask", [P, DM], F32)
            SQ = sb("squares", [P, DM], F32)
            ST8 = sb("x_stats", [P, 10], F32)
        if name in (1, 2):
            G1 = sb("norm_w", [P, 4], F32)
            B1 = sb("norm_b", [P, 4], F32)
            BN = sb("bn", [P, 2, 6], F32)
            MV = sb("mean_var", [P, 2, 2], F32)
            RS = sb("rstd", [P, 2], F32)
        if name == 1:
            GT = sb("gate", [P, 1], F32)
        if name in (2, 3):
            BO = sb("out_bias", [P, DM], F32)
        if name == 3:
            MKF = sb("mask_raw", [P, 2, 2, TOK], F32)
            MKC = sb("mask_clamped", [P, 2, 2, 2, TOK], F32)
            MKS = sb("mask_split", [P, 2, 2, 2, TOK], F32R)
            GA = sb("gamma", [P, DM], F32)
            BE = sb("beta", [P, DM], F32)
            BN = sb("bn", [P, 2, 6], F32)
            MV = sb("mean_var", [P, 2, 2], F32)
            RS = sb("rstd", [P, 2], F32)

        SB = ctx.enter_context(nc.psum_tensor(f"l{name}_scores", [P, 2, BANK], F32))
        AB = ctx.enter_context(nc.psum_tensor(f"l{name}_scores_t", [P, 2, BANK], F32))
        OB = ctx.enter_context(nc.psum_tensor(f"l{name}_out", [P, 2, BANK], F32))
        FB = ctx.enter_context(nc.psum_tensor(f"l{name}_jobs", [P, 2, BANK], F32))

        c_ident = sem("c_ident")
        c_load = sem("c_load")
        c_stacks = sem("c_stacks")
        c_onehot = sem("c_onehot")
        c_pool = sem("c_pool")
        consts = []
        if name != 1:
            consts += [(BQ[:, :], D["bq"]), (BK[:, :], D["bk"]),
                       (BV[:, :], D["bv"].partition_broadcast(P))]
        if name in (1, 2):
            consts += [(G1[:, :], D["ln_w"]), (B1[:, :], D["ln_b"])]
        if name == 1:
            consts += [(GT[:, :], D["gate"].partition_broadcast(P))]
        if name in (2, 3):
            consts += [(BO[:, :], D["bo"].partition_broadcast(P))]
        if name == 3:
            consts += [(GA[:, :], D["gamma"].partition_broadcast(P)),
                       (BE[:, :], D["beta"].partition_broadcast(P))]
        load, high, low = weight_steps(sem, weights, PR[:, :, :, :].rearrange("p a b n -> p (a b) n"))
        with nc.Block() as block:
            @block.gpsimd
            def _(pool):
                pool.memset(IDF[:, :], 0.0).then_inc(c_pool, 1)
                pool.memset(OHF[:, :], 0.0).then_inc(c_pool, 1)
                for n, value in enumerate((-0.5, 1e-6 if name == 3 else 1e-5)):
                    pool.memset(CONST[:, n:n + 1], value)
                pool.wait_ge(c_pool, 2)
                pool.affine_select(out=IDF[:, :], in_=IDF[:, :], compare_op=ALU.not_equal, fill=1.0,
                                   base=0, pattern=[[-1, P]], channel_multiplier=1).then_inc(c_ident, 1)
                pool.affine_select(out=OHF[:, :], in_=OHF[:, :], compare_op=ALU.not_equal, fill=1.0,
                                   base=-(ROW1 + 1), pattern=[[-1, L.rows]], channel_multiplier=1).then_inc(c_ident, 1)
                for par in range(2):
                    pool.memset(KS[:, par, :, :].bitcast(F32), 0.0).then_inc(c_stacks, 1)
                    pool.memset(QS[:, par, :, :].bitcast(F32), 1.0).then_inc(c_stacks, 1)
                pool.memset(NM[:, :, :, :, :].bitcast(F32), 0.0).then_inc(c_pool, 1)
                pool.wait_ge(c_pool, 3)
                pool.memset(NM[:, :, :, :, ROW1:ROW1 + 1].bitcast(F32), 1.0)
                if name == 3:
                    pool.memset(V[:, :, :, :], 0.0)
                    pool.memset(ONES[:, 0:16], 0.0)
                    pool.memset(ONES[:, 16:32], 1.0)
                    pool.memset(ONES[:, 32:48], 0.0)
                else:
                    pool.memset(ONES[:, :], 1.0)

            @block.vector
            def _(dve):
                dve.wait_ge(c_ident, 2)
                dve.tensor_copy(IDR[:, :], IDF[:, :])
                for r in range(L.rows):
                    src = OHF[ROW1:L.depth, r:r + 1].to_broadcast([L.rows + 1, L.keys])
                    dve.tensor_copy(OHR[ROW1:L.depth, r, :], src).then_inc(c_onehot, 1)
                low(dve)

            @block.scalar
            def _(act):
                high(act)
                if name == 1:
                    act.wait_ge(c_load, 16 * (len(consts) + 2 * L.rows))
                    act.activation(GT[:, :], GT[:, :], ACT.Tanh)
                elif name == 3:
                    act.wait_ge(c_load, 16 * (len(consts) + 2 * L.rows))
                    act.activation(BQ[:, :], BQ[:, :], ACT.Copy, scale=0.25)

            @block.sync
            def _(sp):
                for dst, src in consts:
                    sp.dma_start(dst, src).then_inc(c_load, 16)
                load(sp)
                sp.wait_ge(c_onehot, L.rows)
                for par in range(2):
                    sp.wait_ge(c_stacks, 2 * par + 1)
                    for r in range(L.rows):
                        sp.dma_start(
                            words(KS[ROW1:L.depth, par, r:L.kv_heads:L.rows, :]),
                            words(OHR[ROW1:L.depth, r:r + 1, :]).to_broadcast(
                                [L.rows + 1, L.kv_heads // L.rows, L.keys])).then_inc(c_load, 16)
                sp.wait_ge(c_load, 16 * (len(consts) + 2 * L.rows))

        scores_ready = sem("scores_ready")
        maxima_done = sem("maxima_done")
        act_ready = sem("act_ready")
        act_done = sem("act_done")
        sums_ready = sem("sums_ready")
        av_done = sem("av_done")
        recip_done = sem("recip_done")
        norm_done = sem("norm_done")
        job_ready = sem("job_ready")
        bank_free = [sem("bank_free0"), sem("bank_free1")]
        lo_done = sem("lo_done")
        nat_moved = [sem(f"nat_moved{n}") for n in range(SLOTS)]
        in_x, in_c, in_r, in_m = sem("in_x"), sem("in_c"), sem("in_r"), sem("in_m")
        x_hi = sem("x_hi")
        x_lo = sem("x_lo")
        y_stored = sem("y_stored")
        sp_passed, dve_passed = sem("sp_passed"), sem("dve_passed")
        if name == 0:
            gathered = [sem("gathered0"), sem("gathered1")]
            v_ready = sem("v_ready")
            qmask_done = sem("qmask_done")
            masked_done = sem("masked_done")
            sums_done = sem("sums_done")
            xn_done = sem("xn_done")
            xrstd_done = sem("xrstd_done")
            dev_done = sem("dev_done")
            root_done = sem("root_done")
            y_steps = sem("y_steps")
            y_ready = sem("y_ready")
        if name:
            a_hi = sem("a_hi")
            a_lo = sem("a_lo")
        if name in (1, 2):
            ln_done = sem("ln_done")
            rstd_done = sem("rstd_done")
        if name == 2:
            res_biased = sem("res_biased")
        if name == 3:
            m_clamped = sem("m_clamped")
            m_hi = sem("m_hi")
            m_lo = sem("m_lo")
            res_biased = sem("res_biased")
            ln_done = sem("ln_done")
            rstd_done = sem("rstd_done")
        else:
            m_row = sem("m_row")
            m_moved = [sem("m_moved0"), sem("m_moved1")]

        nat_slot = {j: n % SLOTS for n, j in enumerate(x for x in heads_jobs if x[0] in "QK")}
        moves = {j: (24 if j[0] == "K" and name in (0, 3) else 12) for j in nat_slot}
        per_head = [sum(moves[j] for j in nat_slot if nat_slot[j] == n) for n in range(SLOTS)]
        V_JOBS = 2 if name == 0 else 0

        def moved(job, e):
            n, seen = nat_slot[job], 0
            for j in nat_slot:
                if j == job:
                    break
                seen += moves[j] if nat_slot[j] == n else 0
            return 16 * (per_head[n] * e + seen)

        def rows_after(s):
            return (s + 1) % RS_ == 0 and s + 1 < NS

        def is_first(b):
            return isinstance(b, int) and b == 0

        def unit(b, s, k):
            if k < 0:
                return UB * b + (0 if s == 0 else 4 * s - 2 + s // RS_)
            return UB * b + 1 + 4 * s + k + s // RS_ + (1 if rows_after(s) and k >= 2 else 0)

        def scored(s, j):
            if name == 0:
                p, h = s // 2, 2 * (s % 2) + j // 2
                return 2 * (p // 2) + h // 2, (p % 2) * WIN + (j % 2) * P, 4 * (p // 2) + h
            if name == 3:
                return 2 * s + j // 2, 0, 2 * (s // 2) + j % 2
            return 4 * s + j, 0, 4 * s + j

        def transposed(s, j):
            if name == 0:
                p = s // 2
                return 2 * (p // 2) + j // 2, (p % 2) * WIN, 4 * (p // 2) + j, 2 * (s % 2)
            return scored(s, j) + (0,)

        def count_before(jbase, k):
            return jbase // 2 + k // 2 if isinstance(jbase, int) else jbase[1] + k // 2

        def J(jbase):
            return jbase if isinstance(jbase, int) else jbase[0]

        def pe_scores(pe, b, par, s, j):
            qt, q0, kh = scored(s, j)
            wait(pe, maxima_done, 4 * (NS * b + s) + j - 1)
            bank = SB[:, j % 2, :]
            last = None
            for i in range(BANK // L.keys):
                o = bank[:, i * L.keys:(i + 1) * L.keys]
                last = pe.matmul(o, QS[0:ROW1 + 1, par, qt, q0 + i * P:q0 + (i + 1) * P],
                                 KS[0:ROW1 + 1, par, kh, :], start=True, stop=True)
            last.then_inc(scores_ready, 1)

        def pe_rows(pe, b, s):
            wait(pe, act_done, unit(b, s, -1) - 1)
            wait(pe, maxima_done, 4 * (NS * b + s + RS_))
            bank = AB[:, unit(0, s, -1) % 2, :]
            last = None
            for t in range(L.row_tiles):
                for i in range(2):
                    o = bank[0:L.depth, t * WIN + i * P:t * WIN + (i + 1) * P]
                    last = pe.matmul(o, NM[:, (s // RS_) % 2, t, i, :], IDR[:, :], start=True, stop=True)
            last.then_inc(act_ready, 1)

        def pe_scores_t(pe, b, par, s, j):
            v = unit(b, s, j)
            qt, q0, kh, k0 = transposed(s, j)
            fresh = j == 0 and s % RS_ == 0
            wait(pe, act_done, unit(b, s, -1) + 1 if fresh and s == 0 else v - 1)
            bank = AB[:, unit(0, s, j) % 2, :]
            last = None
            for kk in range(2):
                k = k0 + kk
                o = bank[:, kk * WIN:(kk + 1) * WIN]
                last = pe.matmul(o, KS[0:L.depth, par, kh, k * P:(k + 1) * P],
                                 QS[0:L.depth, par, qt, q0:q0 + WIN], start=True, stop=name != 3)
                if name == 3:
                    pe.matmul(o, IDR[:, :], MKS[:, par, HI, k, :], start=False, stop=False)
                    last = pe.matmul(o, IDR[:, :], MKS[:, par, LO, k, :], start=False, stop=True)
            last.then_inc(act_ready, 1)

        def pe_attend(pe, b, par, s, part):
            if part == 0:
                if s % OS == 0:
                    wait(pe, recip_done, NG * b + s // OS)
                wait(pe, act_done, unit(b, s, 3) + 1)
            elif s % OS == 0:
                wait(pe, norm_done, NG * b + s // OS)
            last = None
            for kk in range(2):
                for g in range(4):
                    kh, k0 = transposed(s, g)[2:]
                    side = 16 * (1 - s % 2) if name == 3 else 0
                    lhs = (V[:, par, k0 + kk, 32 * kh + side:32 * kh + side + 32] if part == 1
                           else ONES[:, side:side + 32])
                    last = pe.matmul(OB[32 * g:32 * g + 32, part, 0:WIN], lhs,
                                     PR[:, s % 2, g, kk * WIN:(kk + 1) * WIN],
                                     start=s % OS == 0 and kk == 0, stop=s % OS == OS - 1 and kk == 1,
                                     tile_position=(0, 32 * g))
            last.then_inc(av_done if part == 1 else sums_ready, 1)

        def pe_job(pe, job, k, par, jbase):
            wait(pe, bank_free[k % 2], count_before(jbase, k))
            bank = FB[:, k % 2, :]
            n = int(job[-1])
            last = None
            if job[1] == "T":
                src = XF if job[0] == "X" else CF
                for f in range(2):
                    for t in range(2):
                        c = (2 * n + f) * P
                        last = pe.transpose(bank[:, f * TOK + t * P:f * TOK + (t + 1) * P],
                                            src[:, t, c:c + P], IDF[:, :])
            elif job[0] in "QK":
                w, x = (WQ, XS) if job[0] == "Q" else (WK, CS)
                tiles = 1 if name == 0 or (job[0] == "K" and name == 3) else 2
                width = DM if name == 0 else TOK
                for f in range(tiles):
                    c = (tiles * n + f) * P
                    last = exact_product(pe, bank[:, f * width:(f + 1) * width],
                                         lambda k_, h: w[:, h, k_, c:c + P],
                                         lambda k_, h: x[:, h, k_, :], kin)
            elif job[0] == "V":
                per = {0: TOK, 3: P}.get(name, DM)
                tiles = 1 if per == DM else 2
                for t in range(tiles):
                    k0 = (n * tiles + t) * P
                    last = exact_product(pe, bank[:, t * per:(t + 1) * per],
                                         lambda k_, h: CS[:, h, k_, k0:k0 + P],
                                         lambda k_, h: WV[:, h, k_, :], kin)
            else:
                last = exact_product(pe, bank, lambda k_, h: XS[:, h, k_, n * P:(n + 1) * P],
                                     lambda k_, h: WO[:, h, k_, :], kin)
            last.then_inc(job_ready, 1)

        def order(jobs, first, finish):
            items = [("job", k) for k in range(len(jobs))]
            banks = [("scores", n) for n in range(4 * AHEAD)] if first else []
            done = banks[:2] + ([("attend", 0)] if finish else [])
            banks = banks[2:]
            if len(jobs) <= 2:
                return done + banks + items[:1] + ([("rows", 0)] if first else []) + items[1:]
            slots = len(jobs) - 1
            if name in (1, 2):
                done = items[:1] + [("attend", 0)] + items[1:LEAD]
                items, banks, slots = items[LEAD:], [("scores", n) for n in range(4 * AHEAD)], slots - LEAD
            for n in range(slots):
                done += items[n:n + 1]
                done += banks[len(banks) * n // slots:len(banks) * (n + 1) // slots]
            if first:
                done.append(("rows", 0))
            return done + items[slots:]

        def after_steps(head, final):
            jobs = section_jobs if head else out_jobs
            return jobs, order(jobs, not final, True)

        def pe_prepared(pe, job, e, sbase):
            if job == "O0":
                return
            if name == 0:
                if job == "Q0":
                    wait(pe, x_lo, 2 * e + 2)
            elif job == "XT0":
                if name == 2:
                    wait(pe, ln_done, 4 * e + 4)
                else:
                    wait(pe, in_x, 16 * (e + 1))
            elif job == "CT0":
                wait(pe, ln_done, 4 * e + 4)
            elif job == "Q0":
                wait(pe, lo_done, sbase + split_index["XT1"] + 1)
            elif job == "K0":
                if name == 1:
                    wait(pe, lo_done, sbase + split_index["CT1"] + 1)
                else:
                    wait(pe, x_lo, e + 1)

        def pe_ready(pe, b, it, par):
            for n in range(SLOTS):
                wait(pe, nat_moved[n], 16 * per_head[n] * (b + 1))
            if name == 3:
                wait(pe, m_lo, b + 1)
            else:
                wait(pe, m_moved[par], 16 * (it + 1))

        def pe_section(pe, b, it, par, jbase, sbase, head, final):
            if name == 0:
                wait(pe, v_ready, 2 * (b + 1))
            for s in range(NS):
                for j in range(4):
                    if s + AHEAD < NS:
                        pe_scores(pe, b, par, s + AHEAD, j)
                    pe_scores_t(pe, b, par, s, j)
                    if j == 1 and rows_after(s):
                        pe_rows(pe, b, s + 1)
                    if s > 0 and j % 2:
                        pe_attend(pe, b, par, s - 1, j // 2)
            jobs, items = after_steps(head, final)
            for what, n in items:
                if what == "job":
                    if jobs[n] == "O0":
                        pe.wait_ge(a_lo, NG * (b + 1))
                    pe_prepared(pe, jobs[n], b + 2, sbase)
                    pe_job(pe, jobs[n], n, par, jbase)
                elif what == "attend":
                    for part in range(2):
                        pe_attend(pe, b, par, NS - 1, part)
                elif what == "scores":
                    if n == 0:
                        pe_ready(pe, b + 1, it + par, 1 - par)
                    pe_scores(pe, b + 1, 1 - par, n // 4, n % 4)
                else:
                    pe_rows(pe, b + 1, 0)

        def act_rows(act, b, par, s):
            qt, q0 = transposed(s, 0)[:2]
            act.wait_ge(act_ready, unit(b, s, -1) + 1)
            bank = AB[ROW1:L.depth, unit(0, s, -1) % 2, :]
            sets = L.row_tiles * L.tiles
            out_ = QS[ROW1:L.depth, par, qt:qt + sets, q0:q0 + WIN]
            src = bank[:, 0:L.row_tiles * WIN].rearrange("p (t n) -> p t n", t=L.row_tiles)
            if L.tiles > 1:
                src = src.to_broadcast([L.rows + 1, L.tiles, WIN])
            act.activation(out_, src, ACT.Copy).then_inc(act_done, 1)

        def act_exp(act, b, s, j):
            if j == 0:
                wait(act, av_done, NS * b + s - 1)
            act.wait_ge(act_ready, unit(b, s, j) + 1)
            act.activation(PR[:, s % 2, j, :], AB[:, unit(0, s, j) % 2, :], ACT.Exp,
                           scale=L.scale).then_inc(act_done, 1)

        def act_split(act, job, k, e, jbase, sbase):
            z = split_index[job]
            n = int(job[-1])
            act.wait_ge(job_ready, J(jbase) + k + 1)
            if job in nat_slot:
                wait(act, nat_moved[nat_slot[job]], moved(job, e))
            parts = 1 if name == 0 or (job[0] == "K" and name == 3) else 2
            width = DM if name == 0 else TOK
            for high in (True, False):
                if not high:
                    wait(act, lo_done, sbase + z - (0 if z == 0 and SH % 2 else 1))
                for f in range(parts):
                    cols = slice(f * width, (f + 1) * width)
                    m = parts * n + f
                    bank = FB[:, k % 2, cols]
                    dst = TMP[:, z % 2, cols]
                    if high:
                        hi = split_dst(job)(HI)
                        dst = hi[:, f, :] if job[1] == "T" else hi[:, cols]
                    if job[0] in {1: "XQK", 3: "X"}.get(name, ""):
                        last = act.activation(dst, bank, ACT.Copy)
                    else:
                        bias, scale = ((B1, G1[:, m:m + 1]) if job[1] == "T" else
                                       (BQ, 0.25 if name == 3 else 1.0) if job[0] == "Q" else (BK, 1.0))
                        last = act.activation(dst, bank, ACT.Identity, bias=bias[:, m:m + 1], scale=scale)
            last.then_inc(bank_free[k % 2], 1)

        def act_job(act, job, k, e, par, jbase, sbase, avs):
            if job in split_index:
                act_split(act, job, k, e, jbase, sbase)
            elif job[0] == "V" and name == 1:
                act.wait_ge(job_ready, J(jbase) + k + 1)
                wait(act, av_done, avs)
                act.activation(V[:, par, int(job[1]), :], FB[:, k % 2, :], ACT.Copy).then_inc(bank_free[k % 2], 1)

        def act_load(act, e):
            act.wait_ge(x_lo, 2 * e + 1)
            act.dma_start(CF[:, :, :], ctx_in[e].rearrange("(i p) n -> p i n", p=P)).then_inc(in_c, 16)

        def act_roots(act, b):
            act.wait_ge(dev_done, 4 * (b + 1))
            act.activation(AO[:, 1, :, :], AO[:, 1, :, :], ACT.Relu).then_inc(root_done, 1)
            act.wait_ge(root_done, 2 * b + 1)
            act.activation(AO[:, 1, :, :], AO[:, 1, :, :], ACT.Sqrt).then_inc(root_done, 1)

        def act_section(act, b, it, par, jbase, sbase, head, final):
            for s in range(NS):
                for j in range(4):
                    act_exp(act, b, s, j)
                    if j == 1 and rows_after(s):
                        act_rows(act, b, par, s + 1)
                if name == 0 and s == 1 and not is_first(b):
                    act_roots(act, b - 1)
                if name == 0 and s == 6 and head:
                    act_load(act, b + 2)
                if name == 0 and s >= NS - 6 and s < NS - 1:
                    n = s - (NS - 6)
                    act.wait_ge(masked_done, 2 * (b + 1))
                    wait(act, sums_done, 5 * b + n)
                    src = QM[:, :] if n == 4 else XR[:, n % 2, :]
                    act.activation(SQ[:, :], src, ACT.Square if n in (2, 3) else ACT.Copy,
                                   accum_out=ST8[:, n:n + 1]).then_inc(sums_done, 1)
            jobs, items = after_steps(head, final)
            for what, n in items:
                if what == "job":
                    act_job(act, jobs[n], n, b + 2, par, jbase, sbase, NS * (b + 1))
                elif what == "rows":
                    act_rows(act, b + 1, 1 - par, 0)

        def dve_max(dve, b, par, s, j):
            if j == 0 and s % RS_ == 0:
                if s >= 2 * RS_:
                    dve.wait_ge(act_ready, unit(b, s - 2 * RS_, -1) + 1)
                elif not is_first(b):
                    dve.wait_ge(act_ready, unit(b - 1, NS - 2 * RS_ + s, -1) + 1)
            wait_apart(dve, scores_ready, 4 * (NS * b + s) + j + 1, dve_passed)
            bank = SB[:, j % 2, :]
            first = ROW1 + 1
            if name == 0:
                r = first + 2 * (s % 2) + j // 2
                src, dst = bank, NM[:, (s // 2) % 2, 0, j % 2, r:r + 1]
            elif name == 3:
                for i in range(2):
                    o = bank[:, i * TOK:(i + 1) * TOK]
                    last = dve.tensor_tensor_reduce(
                        out=o, in0=o, in1=MKC[:, par, 0, i, :], scale=-1.0, scalar=3.0e38, op0=ALU.add,
                        op1=ALU.min, accum_out=NM[:, s % 2, j // 2, i, first + j % 2:first + j % 2 + 1])
                last.then_inc(maxima_done, 1)
                return
            else:
                src = bank.rearrange("p (i n) -> p i n", i=2)
                dst = NM[:, s % 2, 0, :, first + j]
            dve.tensor_reduce(dst, src, AX.X, ALU.max, negate=True).then_inc(maxima_done, 1)

        def dve_recip(dve, b, o):
            dve.wait_ge(sums_ready, NS * b + (o + 1) * OS)
            wait(dve, norm_done, NG * b + o)
            dve.reciprocal(RC[:, :], OB[:, 0, 0:WIN]).then_inc(recip_done, 1)

        def dve_out(dve, b, o, jb):
            g = NG * b + o
            dve.wait_ge(recip_done, g + 1)
            dve.wait_ge(av_done, NS * b + (o + 1) * OS)
            if name == 0:
                slot = (o // 2) % 2
                if o % 2 == 0:
                    wait(dve, gathered[slot], 16 * 8 * (2 * b + o // 4))
                dst = AF[:, slot, (o % 2) * WIN:(o % 2 + 1) * WIN]
            else:
                wait(dve, a_lo, g - 1)
                dst = AF[:, o % 2, :]
            dve.tensor_tensor(dst, OB[:, 1, 0:WIN], RC[:, :], ALU.mult).then_inc(norm_done, 1)
            if name:
                wait(dve, job_ready, jb)
                dve.wait_ge(norm_done, g + 1)
                dve.tensor_copy(XS[:, HI, o, :], dst).then_inc(a_hi, 1)

        def split_dst(job):
            n = int(job[-1])
            if job[1] == "T":
                dst = XS if job[0] == "X" else CS
                return lambda h: dst[:, h, 2 * n:2 * n + 2, :]
            return lambda h: NAT[:, nat_slot[job], h, :]

        def shaped(job, ap):
            if job[0] == "K" and name == 3:
                return ap[:, 0:TOK]
            return ap.rearrange("p (f n) -> p f n", f=2) if job[1] == "T" else ap

        def cut(job, ap):
            return ap[:, 0:TOK] if job[0] == "K" and name == 3 else ap

        def dve_value(dve, job, k, e, par, jbase, avs):
            n = int(job[-1])
            dve.wait_ge(job_ready, J(jbase) + k + 1)
            wait(dve, av_done, avs)
            bank = FB[:, k % 2, :]
            if name == 2:
                last = dve.tensor_tensor(V[:, par, n, :], bank, BV[:, :], ALU.add)
            else:
                w = TOK if name == 0 else P
                for t in range(2):
                    dst = V[:, par, 2 * n + t, VPAD:].rearrange("p (h c) -> p h c", c=32)[:, :, 0:16]
                    last = dve.tensor_tensor(dst, bank[:, t * w:(t + 1) * w].rearrange("p (h d) -> p h d", d=16),
                                             BV[:, :].rearrange("p (h d) -> p h d", d=16), ALU.add)
            last.then_inc(bank_free[k % 2], 1)

        def dve_result(dve, b, n, k, jbase):
            dve.wait_ge(job_ready, J(jbase) + k + 1)
            bank, y = FB[:, k % 2, :], XR[:, n, :]
            if name == 1:
                dve.wait_ge(in_r, 16 * (b + 1))
                last = dve.scalar_tensor_tensor(y, bank, GT[:, 0:1], y, ALU.mult, ALU.add)
            else:
                dve.wait_ge(res_biased, b + 1)
                last = dve.tensor_tensor(y, bank, y, ALU.add)
            last.then_inc(bank_free[k % 2], 1)

        def dve_job(dve, job, k, b, e, par, jbase, sbase, avs):
            if job[0] == "O":
                dve_result(dve, b, int(job[1]), k, jbase)
            elif job[0] == "V" and name != 1:
                dve_value(dve, job, k, e, par, jbase, avs)

        def dve_stats(dve, e):
            if name in (1, 2):
                R = CF if name == 1 else XF
                dve.wait_ge(in_c if name == 1 else in_x, 16 * (e + 1))
                for t in range(2):
                    dve.bn_stats(BN[:, t, :], R[:, t, :]).then_inc(ln_done, 1)
                wait_apart(dve, ln_done, 4 * e + 2, dve_passed)
                for t in range(2):
                    last = dve.bn_aggr(MV[:, t, :], BN[:, t, :])
                last.then_inc(ln_done, 1)

        def dve_prepare(dve, e, ite, pare, jfree):
            if name == 0:
                wait(dve, job_ready, jfree)
                dve.wait_ge(in_x, 16 * (e + 1))
                dve.tensor_copy(XS[:, HI, :, :], XF[:, :, :]).then_inc(x_hi, 1)
            elif name in (2, 3):
                wait(dve, job_ready, jfree)
                dve.wait_ge(in_c, 16 * (e + 1))
                dve.tensor_copy(CS[:, HI, :, :], CF[:, :, :].rearrange("p a (c n) -> p (a c) n", n=TOK)
                                ).then_inc(x_hi, 1)
            if name in (1, 2):
                R = CF if name == 1 else XF
                dve.wait_ge(rstd_done, 2 * e + 2)
                for t in range(2):
                    last = dve.tensor_scalar(R[:, t, :], R[:, t, :], MV[:, t, 0:1], RS[:, t:t + 1],
                                             ALU.subtract, ALU.mult)
                last.then_inc(ln_done, 1)
            if name != 3:
                row = slice(ROW1, ROW1 + 1)
                dve.wait_ge(in_m, 16 * (e + 1))
                if not (isinstance(e, int) and e == 0):
                    n_before = ite + pare if not isinstance(ite, int) else (e - 1) // 2 + 1
                    dve.wait_ge(m_moved[1 - pare], 16 * n_before)
                if name != 1:
                    dve.tensor_scalar(MRR[row, :], MU8[row, :], 1.0, -NEG, ALU.subtract,
                                      ALU.mult).then_inc(m_row, 1)
                else:
                    dve.tensor_scalar(MRF[row, :], MU8[row, :], 1.0, 3.0e38, ALU.subtract,
                                      ALU.mult).then_inc(m_row, 1)
                    dve.wait_ge(m_row, 2 * e + 1)
                    dve.tensor_scalar(MRR[row, :], MRF[row, :], 10.0, None, ALU.mult).then_inc(m_row, 1)

        def dve_prepare_ctx(dve, e):
            dve.wait_ge(in_c, 16 * (e + 1))
            dve.tensor_copy(CS[:, HI, :, :], CF[:, :, :]).then_inc(x_hi, 1)

        def dve_clamp(dve, e, pare):
            dve.wait_ge(in_m, 32 * (e + 1))
            wait(dve, m_lo, e)
            dve.tensor_scalar(MKC[:, pare, :, :, :], MKF[:, :, :, :], NEG, None, ALU.max).then_inc(m_clamped, 1)

        def dve_score_mask(dve, e, pare, taken):
            wait(dve, act_ready, taken)
            dve.wait_ge(m_clamped, e + 1)
            dve.tensor_copy(MKS[:, pare, HI, :, :], MKC[:, pare, 1, :, :]).then_inc(m_hi, 1)

        def dve_instance_norm(dve, b):
            base = 7 * b
            dve.wait_ge(sums_done, 5 * (b + 1))
            dve.reciprocal(ST8[:, 4:5], ST8[:, 4:5]).then_inc(xn_done, 1)
            dve.wait_ge(xn_done, base + 1)
            dve.tensor_scalar(ST8[:, 0:4], ST8[:, 0:4], ST8[:, 4:5], None, ALU.mult).then_inc(xn_done, 1)
            dve.wait_ge(xn_done, base + 2)
            dve.tensor_tensor(ST8[:, 6:8], ST8[:, 0:2], ST8[:, 0:2], ALU.mult).then_inc(xn_done, 1)
            dve.wait_ge(xn_done, base + 3)
            dve.tensor_tensor(ST8[:, 6:8], ST8[:, 2:4], ST8[:, 6:8], ALU.subtract).then_inc(xn_done, 1)
            dve.wait_ge(xn_done, base + 4)
            dve.tensor_scalar(ST8[:, 6:8], ST8[:, 6:8], 0.0, 1e-5, ALU.max, ALU.add).then_inc(xn_done, 1)
            dve.wait_ge(xrstd_done, b + 1)
            for i in range(2):
                dve.tensor_scalar(XR[:, i, :], XR[:, i, :], ST8[:, i:i + 1], ST8[:, 8 + i:9 + i],
                                  ALU.subtract, ALU.mult).then_inc(xn_done, 1)

        def dve_final_norm(dve, b):
            for t in range(2):
                dve.bn_stats(BN[:, t, :], XR[:, t, :]).then_inc(ln_done, 1)
            wait_apart(dve, ln_done, 6 * b + 2, dve_passed)
            for t in range(2):
                last = dve.bn_aggr(MV[:, t, :], BN[:, t, :])
            last.then_inc(ln_done, 1)
            dve.wait_ge(rstd_done, 2 * b + 2)
            for t in range(2):
                last = dve.tensor_scalar(XR[:, t, :], XR[:, t, :], MV[:, t, 0:1], RS[:, t:t + 1],
                                         ALU.subtract, ALU.mult)
            last.then_inc(ln_done, 1)
            dve.wait_ge(ln_done, 6 * b + 4)
            dve.tensor_tensor(XR[:, :, :], XR[:, :, :], GA[:, :].unsqueeze(1).to_broadcast([P, 2, DM]),
                              ALU.mult).then_inc(ln_done, 1)
            dve.wait_ge(ln_done, 6 * b + 5)
            dve.tensor_tensor(XR[:, :, :], XR[:, :, :], BE[:, :].unsqueeze(1).to_broadcast([P, 2, DM]),
                              ALU.add).then_inc(ln_done, 1)

        def dve_section(dve, b, it, par, jbase, sbase, head, final):
            prep_at = 1 if NS == 4 else 3
            for s in range(NS):
                for j in range(4):
                    if s + AHEAD < NS:
                        dve_max(dve, b, par, s + AHEAD, j)
                    if s > 0 and s % OS == 0 and j == 2:
                        dve_recip(dve, b, s // OS - 1)
                if s > 0 and s % OS == 0:
                    dve_out(dve, b, s // OS - 1, J(jbase))
                if name == 3 and s == 1 and not is_first(b):
                    for k in range(2):
                        wait_apart(dve, bank_free[k], count_before(jbase, k), dve_passed)
                    dve_final_norm(dve, b - 1)
                if s == 0 and head:
                    dve_stats(dve, b + 2)
                if s == prep_at and head:
                    dve_prepare(dve, b + 2, it + 1, par, J(jbase))
                if s == 8 and name == 0 and head:
                    dve_prepare_ctx(dve, b + 2)
                if s == NS - 7 and name == 0:
                    dve.wait_ge(in_r, 32 * (b + 1))
                    dve.tensor_copy(QM[:, :], QM8[:, :]).then_inc(qmask_done, 1)
                if name == 0 and s == NS - 1:
                    dve_instance_norm(dve, b)
                if name == 3 and s == NS - 2 and head:
                    dve_clamp(dve, b + 2, par)
            if head and name == 3:
                dve_score_mask(dve, b + 2, par, UB * (b + 1))
            jobs, items = after_steps(head, final)
            for what, n in items:
                if what == "job":
                    dve_job(dve, jobs[n], n, b, b + 2, par, jbase, sbase, NS * (b + 1))
                elif what == "attend":
                    dve_recip(dve, b, NG - 1)
                    dve_out(dve, b, NG - 1, J(jbase))
                elif what == "scores":
                    dve_max(dve, b + 1, 1 - par, n // 4, n % 4)

        def pool_lo(pool, job, k, jbase):
            z = split_index[job]
            pool.wait_ge(bank_free[k % 2], count_before(jbase, k) + 1)
            d = split_dst(job)
            pool.tensor_tensor(cut(job, d(LO)), shaped(job, TMP[:, z % 2, :]),
                               cut(job, d(HI)).bitcast(F32), ALU.subtract).then_inc(lo_done, 1)

        def pool_job(pool, job, k, par, jbase, sbase):
            if job in split_index:
                pool_lo(pool, job, k, jbase)
            elif job[0] == "V" and name == 0:
                pool.wait_ge(bank_free[k % 2], count_before(jbase, k) + 1)
                n = int(job[1])
                v = V[:, par, 2 * n:2 * n + 2, :].rearrange("p t (h c) -> p (t h) c", c=32)
                pool.tensor_tensor(v[:, :, 16:32], v[:, :, 0:16], v[:, :, 0:16], ALU.mult).then_inc(v_ready, 1)

        def pool_attended(pool, b, o):
            pool.wait_ge(a_hi, NG * b + o + 1)
            pool.tensor_tensor(XS[:, LO, o, :], AF[:, o % 2, :], XS[:, HI, o, :].bitcast(F32),
                               ALU.subtract).then_inc(a_lo, 1)

        def pool_prepare(pool, e):
            if name in (1, 2):
                pool.wait_ge(ln_done, 4 * e + 3)
                pool.tensor_tensor(RS[:, :], MV[:, :, 1], CONST[:, 1:2].to_broadcast([P, 2]), ALU.add).then_inc(rstd_done, 1)
                pool.wait_ge(rstd_done, 2 * e + 1)
                pool.tensor_tensor(RS[:, :], RS[:, :], CONST[:, 0:1].to_broadcast([P, 2]),
                                   ALU.pow).then_inc(rstd_done, 1)
            if name == 0:
                for n, (s_, r_) in enumerate(((XS, XF), (CS, CF))):
                    pool.wait_ge(x_hi, 2 * e + n + 1)
                    pool.tensor_tensor(s_[:, LO, :, :], r_[:, :, :], s_[:, HI, :, :].bitcast(F32),
                                       ALU.subtract).then_inc(x_lo, 1)
            elif name in (2, 3):
                pool.wait_ge(x_hi, e + 1)
                pool.tensor_tensor(CS[:, LO, :, :], CF[:, :, :].rearrange("p a (c n) -> p (a c) n", n=TOK),
                                   CS[:, HI, :, :].bitcast(F32), ALU.subtract).then_inc(x_lo, 1)

        def pool_mask_lo(pool, e, pare):
            pool.wait_ge(m_hi, e + 1)
            pool.tensor_tensor(MKS[:, pare, LO, :, :], MKC[:, pare, 1, :, :],
                               MKS[:, pare, HI, :, :].bitcast(F32), ALU.subtract).then_inc(m_lo, 1)

        def pool_variances(pool, b, f):
            for slot in range(2):
                pool.wait_ge(gathered[slot], 16 * 8 * (2 * b + f + 1))
            mean, var = AO[:, 0, f, :], AO[:, 1, f, :]
            base = 4 * b + 2 * f
            if f == 0:
                pool.wait_ge(sums_done, 5 * (b + 1))
            else:
                pool.wait_ge(dev_done, base)
            pool.tensor_tensor(SQ[:, :], mean, mean, ALU.mult).then_inc(dev_done, 1)
            pool.wait_ge(dev_done, base + 1)
            pool.tensor_tensor(var, var, SQ[:, :], ALU.subtract).then_inc(dev_done, 1)

        def pool_final_norm(pool, b):
            pool.wait_ge(ln_done, 6 * b + 3)
            pool.tensor_tensor(RS[:, :], MV[:, :, 1], CONST[:, 1:2].to_broadcast([P, 2]), ALU.add).then_inc(rstd_done, 1)
            pool.wait_ge(rstd_done, 2 * b + 1)
            pool.tensor_tensor(RS[:, :], RS[:, :], CONST[:, 0:1].to_broadcast([P, 2]),
                               ALU.pow).then_inc(rstd_done, 1)

        def pool_y(pool, b):
            pool.wait_ge(root_done, 2 * (b + 1))
            pool.tensor_tensor(XR[:, :, :], XR[:, :, :], AO[:, 1, :, :], ALU.mult).then_inc(y_steps, 1)
            pool.wait_ge(y_steps, 2 * b + 1)
            pool.tensor_tensor(XR[:, :, :], XR[:, :, :], AO[:, 0, :, :], ALU.add).then_inc(y_steps, 1)
            pool.wait_ge(y_steps, 2 * (b + 1))
            for n in range(2):
                pool.tensor_tensor(XR[:, n, :], XR[:, n, :], QM[:, :], ALU.mult).then_inc(y_ready, 1)

        def pool_section(pool, b, it, par, jbase, sbase, head, final):
            if name == 0 and not is_first(b):
                pool_y(pool, b - 1)
            if name == 3 and not is_first(b):
                pool_final_norm(pool, b - 1)
            if head:
                pool_prepare(pool, b + 2)
            if name == 0:
                pool.wait_ge(qmask_done, b + 1)
                for i in range(2):
                    pool.tensor_tensor(XR[:, i, :], XR[:, i, :], QM[:, :], ALU.mult).then_inc(masked_done, 1)
                pool.wait_ge(xn_done, 7 * b + 5)
                pool.tensor_tensor(ST8[:, 8:10], ST8[:, 6:8], CONST[:, 0:1].to_broadcast([P, 2]),
                                   ALU.pow).then_inc(xrstd_done, 1)
                pool_variances(pool, b, 0)
            if name:
                for o in range(NG - 1):
                    pool_attended(pool, b, o)
            if name in (2, 3):
                pool.wait_ge(in_r, 16 * (b + 1))
                pool.tensor_tensor(XR[:, :, :], XR[:, :, :], BO[:, :].unsqueeze(1).to_broadcast([P, 2, DM]),
                                   ALU.add).then_inc(res_biased, 1)
            if head and name == 3:
                pool_mask_lo(pool, b + 2, par)
            jobs, items = after_steps(head, final)
            for what, n in items:
                if what == "job":
                    if jobs[n] == "K0" and name == 0:
                        pool_variances(pool, b, 1)
                    pool_job(pool, jobs[n], n, par, jbase, sbase)
                elif what == "attend" and name:
                    pool_attended(pool, b, NG - 1)
            if name == 0 and not jobs:
                pool_variances(pool, b, 1)
        tiles2 = lambda a: a.rearrange("(i p) n -> p i n", p=P)

        def sp_load(sp, e, jfree):
            if name == 0:
                wait_apart(sp, x_lo, 2 * e, sp_passed)
            else:
                wait_apart(sp, job_ready, jfree, sp_passed)
                if name in (2, 3):
                    wait_apart(sp, x_lo, e, sp_passed)
            sp.dma_start(XF[:, :, :], tiles2(x_in[e])).then_inc(in_x, 16)
            if name == 1:
                sp.dma_start(CF[:, :, :], tiles2(ctx_in[e])).then_inc(in_c, 16)
            elif name:
                sp.dma_start(CF[:, :, :].rearrange("p a (c n) -> p (a c) n", n=TOK),
                             D["ctx_t"][e].rearrange("(c p) n -> p c n", p=P)).then_inc(in_c, 16)
            if name == 3:
                wait_apart(sp, m_clamped, e, sp_passed)
                sp.dma_start(MKF[:, 0, :, :], tiles2(D["mask"][e])).then_inc(in_m, 16)
                sp.dma_start(MKF[:, 1, :, :], tiles2(D["mask_t"][e])).then_inc(in_m, 16)
            else:
                wait_apart(sp, m_row, MR * e, sp_passed)
                sp.dma_start(MU8[ROW1:ROW1 + 1, :], D["mask"][e]).then_inc(in_m, 16)

        def sp_mask(sp, e, par):
            if name != 3:
                sp.wait_ge(m_row, MR * (e + 1))
                src = words(MRR[ROW1:ROW1 + 1, :]).unsqueeze(1).to_broadcast([1, L.kv_heads, L.keys])
                sp.dma_start(words(KS[ROW1:ROW1 + 1, par, :, :]), src).then_inc(m_moved[par], 16)

        def sp_move(sp, e, par, sbase, jobs):
            for job in jobs:
                n, slot = int(job[1]), nat_slot[job]
                wait_apart(sp, lo_done, sbase + split_index[job] + 1, sp_passed)
                parts = (HI, LO, HI) if job[0] == "Q" else (HI, HI, LO)
                dst_all = QS if job[0] == "Q" else KS
                for quad, part in enumerate(parts):
                    for r in range(4):
                        if job[0] == "K" and name in (0, 3):
                            for half in range(2):
                                lo_row = 16 * half + 32 * quad
                                head_ = (8 * n if name == 0 else 0) + 2 * r + half
                                sp.dma_start(words(KS[lo_row:lo_row + 16, par, head_, :]), words(
                                    NAT[32 * r + 16 * half:32 * r + 16 * half + 16, slot, part, 0:L.keys])
                                             ).then_inc(nat_moved[slot], 16)
                            continue
                        src = NAT[32 * r:32 * r + 32, slot, part, :]
                        rows = slice(32 * quad, 32 * quad + 32)
                        if name == 0:
                            dst = dst_all[rows, par, 4 * n + r, :]
                        elif name == 3:
                            dst = dst_all[rows, par, 4 * r + 2 * n:4 * r + 2 * n + 2, :]
                            src = src.rearrange("p (f n) -> p f n", f=2)
                        else:
                            dst = dst_all[rows, par, 8 * n + r:8 * n + r + 5:4, :]
                            src = src.rearrange("p (f n) -> p f n", f=2)
                        sp.dma_start(words(dst), words(src)).then_inc(nat_moved[slot], 16)

        def sp_gather(sp, b, q):
            if q == 0:
                wait_apart(sp, y_ready, 2 * b, sp_passed)
            wait_apart(sp, norm_done, NG * b + 2 * q + 2, sp_passed)
            for g in range(4):
                for kind in range(2):
                    r, c = 32 * g + 16 * kind, 64 * (q % 2) + 16 * g
                    sp.dma_start(AO[c:c + 16, kind, q // 2, :],
                                 AF[r:r + 16, q % 2, :]).then_inc(gathered[q % 2], 16)

        def sp_residual(sp, b):
            wait_apart(sp, y_stored, 16 * b, sp_passed)
            sp.dma_start(XR[:, :, :], tiles2(x_in[b])).then_inc(in_r, 16)
            if name == 0:
                wait_apart(sp, y_ready, 2 * b, sp_passed)
                sp.dma_start(QM8[:, :], D["mask_rows"][b].partition_broadcast(P)).then_inc(in_r, 16)

        def sp_store(sp, b, jbase, head):
            if name == 0:
                wait_apart(sp, y_ready, 2 * (b + 1), sp_passed)
            elif name == 3:
                wait_apart(sp, ln_done, 6 * (b + 1), sp_passed)
            else:
                k0 = OUT_AT if head else 0
                for k in (k0, k0 + 1):
                    wait_apart(sp, bank_free[k % 2], count_before(jbase, k) + 1, sp_passed)
            sp.dma_start(tiles2(out[b]), XR[:, :, :]).then_inc(y_stored, 16)

        def sp_next(sp, b, jbase):
            if not (isinstance(b, int) and b + 3 >= NB):
                sp_load(sp, b + 3, J(jbase) + (section_jobs.index("XT1") + 1 if name else 0))

        def sp_section(sp, b, it, par, jbase, sbase, head, final):
            if name == 0:
                for q in range(4):
                    sp_gather(sp, b, q)
            keys = [j for j in nat_slot if j[0] == "K"]
            queries = [j for j in nat_slot if j[0] == "Q"]
            if head:
                if name == 0:
                    sp_next(sp, b, jbase)
                wait_apart(sp, act_ready, UB * (b + 1), sp_passed)
                sp_mask(sp, b + 2, par)
                sp_move(sp, b + 2, par, sbase, queries + keys[:1] if name == 0 else keys)
                if name == 3:
                    sp_move(sp, b + 2, par, sbase, queries)
                if name:
                    sp_next(sp, b, jbase)
            sp_store(sp, b, jbase, head)
            if head:
                if name in (1, 2):
                    sp_move(sp, b + 2, par, sbase, queries)
                elif name == 0:
                    sp_move(sp, b + 2, par, sbase, keys[1:])
            if not final:
                sp_residual(sp, b + 1)

        def sections(eng, section):
            section(eng, 0, 0, 0, 2 * NH, 2 * SH, True, False)
            with eng.Fori(0, (NB - 4) // 2) as i:
                for n in range(2):
                    b = i * 2 + (1 + n)
                    jbase = (b * NJ + 2 * NH, b * (NJ // 2) + NH)
                    section(eng, b, i + n, 1 - n, jbase, b * SH + 2 * SH, True, False)
            b = NB - 3
            section(eng, b, b // 2, 1, 2 * NH + NJ * b, SH * (b + 2), True, False)
            section(eng, b + 1, NB // 2 - 1, 0, 2 * NH + NJ * (b + 1), SH * NB, False, False)
            section(eng, b + 2, NB // 2 - 1, 1, 2 * NH + NJ * (b + 1) + NT, SH * NB, False, True)

        with nc.Block() as block:
            @block.sync
            def _(sp):
                sp_load(sp, 0, 0)
                for e in range(2):
                    sp_load(sp, e + 1, NH * e + (heads_jobs.index("XT1") + 1 if name else 0))
                    sp_mask(sp, e, e)
                    sp_move(sp, e, e, SH * e, list(nat_slot))
                sp_residual(sp, 0)
                sections(sp, sp_section)
                sp.wait_ge(y_stored, 16 * NB)

            @block.tensor
            def _(pe):
                for e in range(2):
                    for k, job in enumerate(heads_jobs):
                        pe_prepared(pe, job, e, SH * e)
                        pe_job(pe, job, k, e, NH * e)
                pe_ready(pe, 0, 0, 0)
                for n in range(4 * AHEAD):
                    pe_scores(pe, 0, 0, n // 4, n % 4)
                pe_rows(pe, 0, 0)
                sections(pe, pe_section)

            @block.scalar
            def _(act):
                for e in range(2):
                    if name == 0:
                        act_load(act, e)
                    for k, job in enumerate(heads_jobs):
                        act_job(act, job, k, e, e, NH * e, SH * e, 0)
                act_rows(act, 0, 0, 0)
                sections(act, act_section)
                if name == 0:
                    act_roots(act, NB - 1)

            @block.vector
            def _(dve):
                for e in range(2):
                    dve_stats(dve, e)
                    dve_prepare(dve, e, 0, e, NH * e)
                    if name == 0:
                        dve_prepare_ctx(dve, e)
                    if name == 3:
                        dve_clamp(dve, e, e)
                        dve_score_mask(dve, e, e, 0)
                    for k, job in enumerate(heads_jobs):
                        dve_job(dve, job, k, 0, e, e, NH * e, SH * e, 0)
                for n in range(4 * AHEAD):
                    dve_max(dve, 0, 0, n // 4, n % 4)
                sections(dve, dve_section)
                if name == 3:
                    for k in range(2):
                        dve.wait_ge(bank_free[k], NJ * NB // 2)
                    dve_final_norm(dve, NB - 1)

            @block.gpsimd
            def _(pool):
                for e in range(2):
                    pool_prepare(pool, e)
                    if name == 3:
                        pool_mask_lo(pool, e, e)
                    for k, job in enumerate(heads_jobs):
                        pool_job(pool, job, k, e, NH * e, SH * e)
                sections(pool, pool_section)
                if name == 0:
                    pool_y(pool, NB - 1)
                if name == 3:
                    pool_final_norm(pool, NB - 1)

        give_back(nc, used)


def feed_forward(nc, NB, A, x_in, out):
    FT = DM // P
    HT = INNER // P
    FJ = HT // 2
    with ExitStack() as ctx:
        def sb(n, shape, dt):
            return ctx.enter_context(nc.sbuf_tensor(f"ff_{n}", shape, dt))

        used = []

        def sem(n):
            used.append(ctx.enter_context(nc.semaphore(f"ff_{n}")))
            return used[-1]

        WF = sb("fc", [P, 2, FT, INNER], F32R)
        WP = sb("proj", [P, 2, HT, DM], F32R)
        XF = sb("x_raw", [P, 2, DM], F32)
        XR = sb("x_residual", [P, 2, 2, DM], F32)
        XT = sb("x_transposed", [P, 2, DM], F32)
        XS = sb("x_split", [P, 2, FT, TOK], F32R)
        HF = sb("hidden_raw", [P, 4, BANK], F32)
        HS = sb("hidden_split", [P, 2, HT, TOK], F32R)
        IDF = sb("ident", [P, P], F32)
        CONST = sb("constants", [P, 2], F32)
        G2 = sb("norm_w", [P, FT], F32)
        B2 = sb("norm_b", [P, FT], F32)
        BF = sb("fc_bias", [P, HT], F32)
        BP = sb("proj_bias", [P, DM], F32)
        BN = sb("bn", [P, 2, 6], F32)
        MV = sb("mean_var", [P, 2, 2], F32)
        RS = sb("rstd", [P, 2], F32)
        HB = ctx.enter_context(nc.psum_tensor("ff_hidden", [P, 4, BANK], F32))
        TB = ctx.enter_context(nc.psum_tensor("ff_transposed", [P, 2, BANK], F32))
        YB = ctx.enter_context(nc.psum_tensor("ff_out", [P, 2, BANK], F32))

        c_load, c_set = sem("c_load"), sem("c_set")
        consts = [(G2[:, :], A["w4_ln_w"]), (B2[:, :], A["w4_ln_b"]), (BF[:, :], A["w4_fc_b"]),
                  (BP[:, :], A["w4_proj_b"].partition_broadcast(P))]
        fc = A["w4_fc"].rearrange("(k p) n -> p k n", p=P)
        parts = [(fc[:, :, q * DM:(q + 1) * DM], WF[:, :, :, q * DM:(q + 1) * DM]) for q in range(INNER // DM)]
        parts.append((A["w4_proj"].rearrange("(k p) n -> p k n", p=P), WP))
        load, high, low = weight_steps(sem, parts, HF)
        with nc.Block() as block:
            @block.gpsimd
            def _(pool):
                pool.memset(IDF[:, :], 0.0).then_inc(c_set, 1)
                pool.memset(CONST[:, 0:1], -0.5)
                pool.memset(CONST[:, 1:2], 1e-5)
                pool.wait_ge(c_set, 1)
                pool.affine_select(out=IDF[:, :], in_=IDF[:, :], compare_op=ALU.not_equal, fill=1.0,
                                   base=0, pattern=[[-1, P]], channel_multiplier=1).then_inc(c_set, 1)

            @block.sync
            def _(sp):
                for dst, src in consts:
                    sp.dma_start(dst, src).then_inc(c_load, 16)
                load(sp)
                sp.wait_ge(c_load, 16 * len(consts))

            @block.scalar
            def _(act):
                high(act)

            @block.vector
            def _(dve):
                low(dve)

        in_x = sem("in_x")
        in_r = [sem("in_r0"), sem("in_r1")]
        y_stored = [sem("y_stored0"), sem("y_stored1")]
        sp_passed, dve_passed = sem("sp_passed"), sem("dve_passed")
        ln_done = sem("ln_done")
        rstd_done = sem("rstd_done")
        xt_ready = sem("xt_ready")
        xt_taken = sem("xt_taken")
        x_hi, x_lo = sem("x_hi"), sem("x_lo")
        fc_ready = sem("fc_ready")
        gelu_done = sem("gelu_done")
        g_hi, g_lo = sem("g_hi"), sem("g_lo")
        res_biased = sem("res_biased")
        y_ready = sem("y_ready")
        y_done = sem("y_done")
        rows = lambda a: a.rearrange("(i p) n -> p i n", p=P)

        def pair(ap):
            return ap.rearrange("p (f n) -> p f n", f=2)

        def pe_transpose(pe, e):
            pe.wait_ge(ln_done, 4 * (e + 1))
            for n in range(2):
                wait(pe, xt_taken, 2 * e + n - 1)
                for f in range(2):
                    for t in range(2):
                        c = (2 * n + f) * P
                        last = pe.transpose(TB[:, n, f * TOK + t * P:f * TOK + (t + 1) * P],
                                            XF[:, t, c:c + P], IDF[:, :])
                last.then_inc(xt_ready, 1)

        def pe_section(pe, b, it, par, more):
            pe.wait_ge(x_lo, 2 * (b + 1))
            for m in range(FJ):
                wait(pe, gelu_done, FJ * b + m - 3)
                for f in range(2):
                    c = (2 * m + f) * P
                    last = exact_product(pe, HB[:, m % 4, f * TOK:(f + 1) * TOK],
                                         lambda k, h: WF[:, h, k, c:c + P],
                                         lambda k, h: XS[:, h, k, :], FT)
                last.then_inc(fc_ready, 1)
            if more:
                pe_transpose(pe, b + 1)
            for n in range(2):
                wait(pe, y_done, 2 * b + n - 1)
                for k in range(HT):
                    if n == 0 and k % 2 == 0:
                        pe.wait_ge(g_lo, FJ * b + k // 2 + 1)
                    last = exact_product(pe, YB[:, n, :], lambda _, h: HS[:, h, k, n * P:(n + 1) * P],
                                         lambda _, h: WP[:, h, k, :], 1, start=k == 0, stop=k == HT - 1)
                last.then_inc(y_ready, 1)

        def act_transposed(act, e):
            for n in range(2):
                act.wait_ge(xt_ready, 2 * e + n + 1)
                wait(act, x_lo, 2 * e + n - 1)
                for f in range(2):
                    m = 2 * n + f
                    last = act.activation(XT[:, n, f * TOK:(f + 1) * TOK], TB[:, n, f * TOK:(f + 1) * TOK],
                                          ACT.Identity, bias=B2[:, m:m + 1], scale=G2[:, m:m + 1])
                last.then_inc(xt_taken, 1)

        def act_section(act, b, it, par, more):
            for m in range(FJ):
                act.wait_ge(fc_ready, FJ * b + m + 1)
                wait(act, g_lo, FJ * b + m - 3)
                for f in range(2):
                    h = 2 * m + f
                    last = act.activation(HF[:, m % 4, f * TOK:(f + 1) * TOK],
                                          HB[:, m % 4, f * TOK:(f + 1) * TOK],
                                          ACT.Gelu_apprx_tanh, bias=BF[:, h:h + 1])
                last.then_inc(gelu_done, 1)
            if more:
                act_transposed(act, b + 1)

        def dve_norm(dve, e):
            dve.wait_ge(in_x, 16 * (e + 1))
            for t in range(2):
                dve.bn_stats(BN[:, t, :], XF[:, t, :]).then_inc(ln_done, 1)
            wait_apart(dve, ln_done, 4 * e + 2, dve_passed)
            for t in range(2):
                last = dve.bn_aggr(MV[:, t, :], BN[:, t, :])
            last.then_inc(ln_done, 1)
            dve.wait_ge(rstd_done, 2 * e + 2)
            for t in range(2):
                last = dve.tensor_scalar(XF[:, t, :], XF[:, t, :], MV[:, t, 0:1], RS[:, t:t + 1],
                                         ALU.subtract, ALU.mult)
            last.then_inc(ln_done, 1)

        def dve_transposed(dve, e):
            for n in range(2):
                dve.wait_ge(xt_taken, 2 * e + n + 1)
                dve.tensor_copy(XS[:, HI, 2 * n:2 * n + 2, :], pair(XT[:, n, :])).then_inc(x_hi, 1)

        def dve_section(dve, b, it, par, more):
            for m in range(FJ):
                dve.wait_ge(gelu_done, FJ * b + m + 1)
                if m == 0:
                    wait(dve, y_ready, 2 * b)
                dve.tensor_copy(HS[:, HI, 2 * m:2 * m + 2, :], pair(HF[:, m % 4, :])).then_inc(g_hi, 1)
                if m == 3 and more:
                    dve_norm(dve, b + 1)
            if more:
                dve_transposed(dve, b + 1)
            dve.wait_ge(res_biased, b + 1)
            for n in range(2):
                dve.wait_ge(y_ready, 2 * b + n + 1)
                dve.tensor_tensor(XR[:, par, n, :], YB[:, n, :], XR[:, par, n, :], ALU.add).then_inc(y_done, 1)

        def pool_norm(pool, e):
            pool.wait_ge(ln_done, 4 * e + 3)
            pool.tensor_tensor(RS[:, :], MV[:, :, 1], CONST[:, 1:2].to_broadcast([P, 2]), ALU.add).then_inc(rstd_done, 1)
            pool.wait_ge(rstd_done, 2 * e + 1)
            pool.tensor_tensor(RS[:, :], RS[:, :], CONST[:, 0:1].to_broadcast([P, 2]), ALU.pow).then_inc(rstd_done, 1)

        def pool_transposed(pool, e):
            for n in range(2):
                pool.wait_ge(x_hi, 2 * e + n + 1)
                pool.tensor_tensor(XS[:, LO, 2 * n:2 * n + 2, :], pair(XT[:, n, :]),
                                   XS[:, HI, 2 * n:2 * n + 2, :].bitcast(F32), ALU.subtract).then_inc(x_lo, 1)

        def pool_section(pool, b, it, par, more):
            for m in range(FJ):
                pool.wait_ge(g_hi, FJ * b + m + 1)
                pool.tensor_tensor(HS[:, LO, 2 * m:2 * m + 2, :], pair(HF[:, m % 4, :]),
                                   HS[:, HI, 2 * m:2 * m + 2, :].bitcast(F32), ALU.subtract).then_inc(g_lo, 1)
                if m == 3 and more:
                    pool_norm(pool, b + 1)
            if more:
                pool_transposed(pool, b + 1)
            pool.wait_ge(in_r[par], 16 * (it + 1))
            pool.tensor_tensor(XR[:, par, :, :], XR[:, par, :, :],
                               BP[:, :].unsqueeze(1).to_broadcast([P, 2, DM]), ALU.add).then_inc(res_biased, 1)

        def sp_section(sp, b, it, par, more):
            if more:
                wait_apart(sp, xt_ready, 2 * (b + 1), sp_passed)
                sp.dma_start(XF[:, :, :], rows(x_in[b + 1])).then_inc(in_x, 16)
            wait_apart(sp, y_stored[par], 16 * it, sp_passed)
            sp.dma_start(XR[:, par, :, :], rows(x_in[b])).then_inc(in_r[par], 16)
            wait_apart(sp, y_done, 2 * (b + 1), sp_passed)
            sp.dma_start(rows(out[b]), XR[:, par, :, :]).then_inc(y_stored[par], 16)

        def sections(eng, section):
            for par in range(2):
                section(eng, par, 0, par, True)
            with eng.Fori(1, NB // 2 - 1) as it:
                for par in range(2):
                    section(eng, it * 2 + par, it, par, True)
            section(eng, NB - 2, NB // 2 - 1, 0, True)
            section(eng, NB - 1, NB // 2 - 1, 1, False)

        with nc.Block() as block:
            @block.sync
            def _(sp):
                sp.dma_start(XF[:, :, :], rows(x_in[0])).then_inc(in_x, 16)
                sections(sp, sp_section)
                for par in range(2):
                    sp.wait_ge(y_stored[par], 16 * (NB // 2))

            @block.tensor
            def _(pe):
                pe_transpose(pe, 0)
                sections(pe, pe_section)

            @block.scalar
            def _(act):
                act_transposed(act, 0)
                sections(act, act_section)

            @block.vector
            def _(dve):
                dve_norm(dve, 0)
                dve_transposed(dve, 0)
                sections(dve, dve_section)

            @block.gpsimd
            def _(pool):
                pool_norm(pool, 0)
                pool_transposed(pool, 0)
                sections(pool, pool_section)

        give_back(nc, used)


def views(layer, A):
    w = f"w{layer}_"
    D = {n: A[w + n] for n in ("wq", "wk", "wv")}
    if layer:
        D["wo"] = A[w + "wo"]
    if layer != 1:
        for n in ("bq", "bk", "bv"):
            D[n] = A[w + n]
    if layer == 0:
        D["mask"], D["mask_rows"] = A["mask_row"], A["mask_row"].rearrange("b a n -> b (a n)")
    elif layer in (1, 2):
        D["mask"] = A["key_mask"]
        D["ln_w"], D["ln_b"] = A[w + "ln_w"], A[w + "ln_b"]
    if layer == 1:
        D["gate"] = A[w + "gate"]
    if layer in (2, 3):
        D["bo"], D["ctx_t"] = A[w + "bo"], A["ctx_t"]
    if layer == 3:
        D["gamma"], D["beta"] = A[w + "gamma"], A[w + "beta"]
        D["mask"], D["mask_t"] = A["mask"], A["mask_t"]
    return D


def layouts(inputs):
    a = {k: np.asarray(v) for k, v in inputs.items()}
    c = np.ascontiguousarray
    cols = lambda v: c(v.reshape(-1, P).T)
    nb = a["x"].shape[0]
    by_member = lambda w: w.reshape(w.shape[:-1] + (8, 4, 16)).swapaxes(-3, -2).reshape(w.shape)
    by_output = lambda w: w.reshape(4, 2, 2, 2, 16, -1).transpose(0, 3, 1, 2, 4, 5).reshape(w.shape)
    out = {
        "x": c(a["x"]), "ctx": c(a["ctx_2048"]), "ctx_t": c(a["ctx_2048"].transpose(0, 2, 1)),
        "mask_row": c(a["mask_Bx1x2048_bf1"].view(np.uint8)),
        "key_mask": c(a["mask_BxS2_bf1"].view(np.uint8).reshape(nb, 1, -1)),
        "mask": c(a["mask_Bx1xSxS2_ff0"][:, 0]), "mask_t": c(a["mask_Bx1xSxS2_ff0"][:, 0].transpose(0, 2, 1)),
        "w0_wq": c(a["L0_xattn_Wq"].T), "w0_wk": c(a["L0_xattn_Wk"].T), "w0_wv": c(a["L0_xattn_Wv"].T),
        "w0_bq": cols(a["L0_xattn_bq"]), "w0_bk": cols(a["L0_xattn_bk"]), "w0_bv": c(a["L0_xattn_bv"]),
        "w1_wq": c(a["L1_xattn_Wq"].T), "w1_wk": c(a["L1_xattn_Wk"].T), "w1_wv": c(a["L1_xattn_Wv"].T),
        "w1_wo": c(a["L1_xattn_Wo"].T), "w1_ln_w": cols(a["L1_xattn_ln_gamma"]),
        "w1_ln_b": cols(a["L1_xattn_ln_beta"]), "w1_gate": c(a["L1_xattn_gate"]),
        "w2_wq": c(a["L2_xattn_q_w"]), "w2_wk": c(a["L2_xattn_k_w"]), "w2_wv": c(a["L2_xattn_v_w"]),
        "w2_wo": c(a["L2_xattn_cproj_w"]), "w2_bq": cols(a["L2_xattn_q_b"]), "w2_bk": cols(a["L2_xattn_k_b"]),
        "w2_bv": c(a["L2_xattn_v_b"]), "w2_bo": c(a["L2_xattn_cproj_b"]),
        "w2_ln_w": cols(a["L2_xattn_ln1_w"]), "w2_ln_b": cols(a["L2_xattn_ln1_b"]),
        "w4_ln_w": cols(a["L2_xattn_ln2_w"]), "w4_ln_b": cols(a["L2_xattn_ln2_b"]),
        "w4_fc": c(a["L2_xattn_fc_w"]), "w4_fc_b": cols(a["L2_xattn_fc_b"]),
        "w4_proj": c(a["L2_xattn_proj_w"]), "w4_proj_b": c(a["L2_xattn_proj_b"]),
        "w3_wq": c(by_member(a["L3_xattn_Wq"])), "w3_wk": c(a["L3_xattn_Wk"]), "w3_wv": c(a["L3_xattn_Wv"]),
        "w3_wo": c(by_output(a["L3_xattn_Wo"])), "w3_bq": cols(by_member(a["L3_xattn_bq"])),
        "w3_bk": cols(a["L3_xattn_bk"]), "w3_bv": c(a["L3_xattn_bv"]), "w3_bo": c(a["L3_xattn_bo"]),
        "w3_gamma": c(a["L3_xattn_gamma"]), "w3_beta": c(a["L3_xattn_beta"]),
    }
    return out


def build(nc, NB, A, out):
    shape = (NB, TOK, DM)
    x1 = nc.dram_tensor("x_after_layer0", shape, F32, kind="Internal").ap()
    x2 = nc.dram_tensor("x_after_layer1", shape, F32, kind="Internal").ap()
    x3 = nc.dram_tensor("x_after_attention2", shape, F32, kind="Internal").ap()
    x4 = nc.dram_tensor("x_after_layer2", shape, F32, kind="Internal").ap()
    attention_layer(nc, L0, NB, views(0, A), A["x"], A["ctx"], x1)
    attention_layer(nc, L1, NB, views(1, A), x1, A["ctx"], x2)
    attention_layer(nc, L2, NB, views(2, A), x2, A["ctx"], x3)
    feed_forward(nc, NB, A, x3, x4)
    attention_layer(nc, L3, NB, views(3, A), x4, A["ctx"], out)


def kernel(**inputs):
    from concourse import bacc, mybir as _mybir
    from concourse.bass_utils import run_bass_kernel_spmd
    arrays = layouts(inputs)
    nb = arrays["x"].shape[0]
    nc = bacc.Bacc("TRN2", target_bir_lowering=False, num_devices=1)
    A = {n: nc.dram_tensor(n, a.shape, _mybir.dt.from_np(a.dtype), kind="ExternalInput").ap()
         for n, a in arrays.items()}
    out = nc.dram_tensor("out", (nb, TOK, DM), F32, kind="ExternalOutput").ap()
    build(nc, nb, A, out)
    result = run_bass_kernel_spmd(nc, [arrays], core_ids=[0])
    return result.results[0]["out"]
```
